# Optimizing a Trainium2 kernel written in Bass

```python
import numpy as np
import jax
import jax.numpy as jnp

def _softmax(x, axis=-1):
    return jax.nn.softmax(x, axis=axis)

def _gelu(x):
    return jax.nn.gelu(x, approximate=True)

def _silu(x):
    return jax.nn.silu(x)

def _sigmoid(x):
    return jax.nn.sigmoid(x)

def _layernorm(x, axis=-1, eps=1e-05):
    m = jnp.mean(x, axis=axis, keepdims=True)
    v = jnp.var(x, axis=axis, keepdims=True)
    return (x - m) / jnp.sqrt(v + eps)

def _scatter_add(tgt, idx, src, axis=0):
    return tgt.at[idx].add(src)

def _segment_sum(src, seg, n):
    return jax.ops.segment_sum(src, seg, n)
kernel_name = 'mk_xattn_ffn_d1_seqx_r2_265ded'

def setup_inputs(seed: int=0):
    np.random.seed(seed)
    _w = jnp.asarray

    def _rec_inputs():
        import jax
        import jax.numpy as jnp
        _rk = jax.random.key(seed)
        x = -0.0003929 + 0.9999 * jax.random.normal(jax.random.fold_in(_rk, 1), (2, 2048, 512), jnp.float32)
        _lenS = 2048 - jax.random.randint(jax.random.fold_in(_rk, 7), (2,), 0, max(1, 2048 // 4) + 1, jnp.int32)
        _lenS2 = 77 - jax.random.randint(jax.random.fold_in(_rk, 8), (2,), 0, max(1, 77 // 4) + 1, jnp.int32)
        _ctx_768P = jax.random.normal(jax.random.fold_in(_rk, 11), (2, 16, 384), jnp.float32)
        _ctx_768c = jax.random.dirichlet(jax.random.fold_in(_rk, 511), 0.3 * jnp.ones((16,), jnp.float32), (2, 77))
        _ctx_768t = jnp.einsum('bsk,bkd->bsd', _ctx_768c, _ctx_768P)
        _ctx_768t = _ctx_768t * jax.lax.rsqrt(jnp.mean(jnp.square(_ctx_768t)) + 1e-12) * 0.953939
        ctx_768 = -0.00055796 + 0.999787 * (_ctx_768t + 0.3 * jax.random.normal(jax.random.fold_in(_rk, 611), (2, 77, 384), jnp.float32))
        return (x, ctx_768)
    x, ctx_768 = _rec_inputs()

    def _L0_xattn_setup():
        import jax, jax.numpy as jnp
        import numpy as np
        D = 512
        L = 384
        H = 16
        EPS = 1e-05

        def layer_norm(x, g, b):
            mu = jnp.mean(x, axis=-1, keepdims=True)
            var = jnp.var(x, axis=-1, keepdims=True)
            return (x - mu) * jax.lax.rsqrt(var + EPS) * g + b
        key = jax.random.key(seed)
        ks = jax.random.split(key, 8)
        B, T, N = (4, 2048, 256)
        sq = lambda d: 1.0 / np.sqrt(d)
        return {'x': jax.random.normal(ks[0], (B, T, D), jnp.float32), 'xf': jax.random.normal(ks[1], (B, N, L), jnp.float32), 'norm_g': jnp.ones((D,), jnp.float32), 'norm_b': jnp.zeros((D,), jnp.float32), 'tnorm_g': jnp.ones((L,), jnp.float32), 'tnorm_b': jnp.zeros((L,), jnp.float32), 'Wq': jax.random.normal(ks[2], (D, D), jnp.float32) * sq(D), 'bq': jnp.zeros((D,), jnp.float32), 'Wk': jax.random.normal(ks[3], (L, D), jnp.float32) * sq(L), 'bk': jnp.zeros((D,), jnp.float32), 'Wv': jax.random.normal(ks[4], (L, D), jnp.float32) * sq(L), 'bv': jnp.zeros((D,), jnp.float32)}
    _L0_xattn_all = _L0_xattn_setup()
    _L0_xattn_in = {k: v for k, v in _L0_xattn_all.items() if k in ('norm_g', 'norm_b', 'tnorm_g', 'tnorm_b', 'Wq', 'bq', 'Wk', 'bk', 'Wv', 'bv')}
    del _L0_xattn_all

    def _L0_ffn_setup():
        import jax, jax.numpy as jnp
        import numpy as np
        D_MODEL, D_FF, RANK = (512, 2048, 128)
        B, S = (4, 2048)
        key = jax.random.key(seed)
        ks = jax.random.split(key, 7)
        return {'x': jax.random.normal(ks[0], (B, S, D_MODEL), dtype=jnp.float32), 'U1': jax.random.normal(ks[1], (D_MODEL, RANK), dtype=jnp.float32) * 0.02, 'V1': jax.random.normal(ks[2], (RANK, D_FF), dtype=jnp.float32) * 0.02, 'b1': jnp.zeros((D_FF,), dtype=jnp.float32), 'U2': jax.random.normal(ks[3], (D_FF, RANK), dtype=jnp.float32) * 0.02, 'V2': jax.random.normal(ks[4], (RANK, D_MODEL), dtype=jnp.float32) * 0.02, 'b2': jnp.zeros((D_MODEL,), dtype=jnp.float32)}
    _L0_ffn_all = _L0_ffn_setup()
    _L0_ffn_in = {k: v for k, v in _L0_ffn_all.items() if k in ('U1', 'V1', 'b1', 'U2', 'V2', 'b2')}
    del _L0_ffn_all
    return {'x': x, 'ctx_768': ctx_768, 'L0_xattn_norm_g': _L0_xattn_in['norm_g'], 'L0_xattn_norm_b': _L0_xattn_in['norm_b'], 'L0_xattn_tnorm_g': _L0_xattn_in['tnorm_g'], 'L0_xattn_tnorm_b': _L0_xattn_in['tnorm_b'], 'L0_xattn_Wq': _L0_xattn_in['Wq'], 'L0_xattn_bq': _L0_xattn_in['bq'], 'L0_xattn_Wk': _L0_xattn_in['Wk'], 'L0_xattn_bk': _L0_xattn_in['bk'], 'L0_xattn_Wv': _L0_xattn_in['Wv'], 'L0_xattn_bv': _L0_xattn_in['bv'], 'L0_ffn_U1': _L0_ffn_in['U1'], 'L0_ffn_V1': _L0_ffn_in['V1'], 'L0_ffn_b1': _L0_ffn_in['b1'], 'L0_ffn_U2': _L0_ffn_in['U2'], 'L0_ffn_V2': _L0_ffn_in['V2'], 'L0_ffn_b2': _L0_ffn_in['b2']}

def reference(x, ctx_768, L0_xattn_norm_g, L0_xattn_norm_b, L0_xattn_tnorm_g, L0_xattn_tnorm_b, L0_xattn_Wq, L0_xattn_bq, L0_xattn_Wk, L0_xattn_bk, L0_xattn_Wv, L0_xattn_bv, L0_ffn_U1, L0_ffn_V1, L0_ffn_b1, L0_ffn_U2, L0_ffn_V2, L0_ffn_b2):
    import jax
    import jax.numpy as jnp

    def _L0_xattn_ref(x, xf, norm_g, norm_b, tnorm_g, tnorm_b, Wq, bq, Wk, bk, Wv, bv):
        import jax, jax.numpy as jnp
        import numpy as np
        D = 512
        L = 384
        H = 16
        EPS = 1e-05

        def layer_norm(x, g, b):
            mu = jnp.mean(x, axis=-1, keepdims=True)
            var = jnp.var(x, axis=-1, keepdims=True)
            return (x - mu) * jax.lax.rsqrt(var + EPS) * g + b
        B, T, _ = x.shape
        N = xf.shape[1]
        hd = D // H
        xn = layer_norm(x, norm_g, norm_b)
        xfn = layer_norm(xf, tnorm_g, tnorm_b)
        q = (xn @ Wq + bq).reshape(B, T, H, hd)
        k = (xfn @ Wk + bk).reshape(B, N, H, hd)
        v = (xfn @ Wv + bv).reshape(B, N, H, hd)
        scores = jnp.einsum('bthd,bnhd->bhtn', q, k) / jnp.sqrt(jnp.float32(hd))
        w = jax.nn.softmax(scores, axis=-1)
        y = jnp.einsum('bhtn,bnhd->bthd', w, v).reshape(B, T, D)
        return y

    def _L0_ffn_ref(x, U1, V1, b1, U2, V2, b2):
        import jax, jax.numpy as jnp
        import numpy as np
        D_MODEL, D_FF, RANK = (512, 2048, 128)
        B, S = (4, 2048)
        P = jnp.einsum('bsd,dr->bsr', x, U1)
        H = jax.nn.gelu(jnp.einsum('bsr,rf->bsf', P, V1) + b1)
        Q = jnp.einsum('bsf,fr->bsr', H, U2)
        return jnp.einsum('bsr,rd->bsd', Q, V2) + b2
    x = x + _L0_xattn_ref(_layernorm(x, axis=-1), ctx_768, L0_xattn_norm_g, L0_xattn_norm_b, L0_xattn_tnorm_g, L0_xattn_tnorm_b, L0_xattn_Wq, L0_xattn_bq, L0_xattn_Wk, L0_xattn_bk, L0_xattn_Wv, L0_xattn_bv)
    x = x + _L0_ffn_ref(_layernorm(x, axis=-1), L0_ffn_U1, L0_ffn_V1, L0_ffn_b1, L0_ffn_U2, L0_ffn_V2, L0_ffn_b2)
    return x

_drawn_inputs = setup_inputs


def setup_inputs(seed=0):
    import zlib

    import numpy as np

    out = dict(_drawn_inputs(seed))
    spreads = {'L0_xattn_norm_g': (1.0, 0.2),
     'L0_xattn_norm_b': (0.0, 0.476),
     'L0_xattn_tnorm_g': (1.0, 0.2),
     'L0_xattn_tnorm_b': (0.0, 0.1),
     'L0_xattn_bq': (0.0, 0.476),
     'L0_xattn_bk': (0.0, 2.0),
     'L0_xattn_bv': (0.0, 0.1),
     'L0_ffn_b1': (0.0, 0.8),
     'L0_ffn_b2': (0.0, 0.8)}
    factors = {'L0_ffn_U1': 6.289, 'L0_ffn_V1': 6.251, 'L0_ffn_U2': 4.494, 'L0_ffn_V2': 4.735}
    for name, (base, spread) in spreads.items():
        noise = np.random.default_rng([zlib.crc32(name.encode()), seed]).standard_normal(out[name].shape)
        drawn = base * np.exp(spread * noise) if base else spread * noise
        out[name] = jnp.asarray(drawn.astype(out[name].dtype))
    for name, factor in factors.items():
        out[name] = (out[name] * factor).astype(out[name].dtype)
    return out
```

```python
from contextlib import ExitStack

import concourse.bass as bass
from concourse import mybir

ALU = mybir.AluOpType
ACT = mybir.ActivationFunctionType
AX = mybir.AxisListType
F32 = mybir.dt.float32
F32R = mybir.dt.float32r
F16 = mybir.dt.float16
BF16 = mybir.dt.bfloat16

P = 128
EPS = 1e-5
HEADS = 16
LAG = 3
DMA = 16


def at_least(eng, sem, value):
    if isinstance(value, int) and value <= 0:
        return
    eng.wait_ge(sem, value)


def xattn_ffn(nc, x, ctx, norm_g, norm_b, tnorm_g, tnorm_b, Wq, bq, Wk, bk, Wv, bv,
              U1, V1, b1, U2, V2, b2, out):
    B, T, D = x.shape
    N, L = ctx.shape[1], ctx.shape[2]
    HD = D // HEADS
    RANK, F = V1.shape
    assert D == 512 and RANK == P and HD == 32
    DC, LC, FC = D // P, L // P, F // P
    TB = 512
    TT = TB // P
    BLOCKS = B * T // TB
    PER_B = T // TB
    G = HEADS // 4
    J = 4
    KS = 3 * HD + 2
    VW = HD + 1
    HALF = HEADS // 2
    SCALE = float(HD) ** -0.5

    xf = x.rearrange("b t d -> (b t) d")
    of = out.rearrange("b t d -> (b t) d")

    with ExitStack() as stack:
        def sb(name, shape, dt=F32):
            return stack.enter_context(nc.sbuf_tensor(name, shape, dt))

        def psum(name):
            return stack.enter_context(nc.psum_tensor(name, [P, 512], F32))

        def sem(name):
            return stack.enter_context(nc.semaphore(name))

        wq = sb("wq", [P, 2, DC, D], F32R)
        u1 = sb("u1", [P, 2, DC, RANK], F32R)
        v1 = sb("v1", [P, 2, F], F32R)
        u2 = sb("u2", [P, 2, FC, RANK], F32R)
        v2 = sb("v2", [P, 2, D], F32R)
        bqs = sb("bqs", [P, DC])
        b1s = sb("b1s", [P, FC])
        q_bias = sb("q_bias", [P, DC])
        b2_all = sb("b2_all", [P, D])
        ident = sb("ident", [P, P])
        mhalf = sb("mhalf", [P, TT])
        xa = sb("xa", [P, TT, D])
        x1 = sb("x1", [P, TT, D])
        xn = sb("xn", [P, TT, D])
        ytmp = sb("ytmp", [P, 2, D])
        xt = sb("xt", [P, 2, DC, TB], F32R)
        qh = sb("qh", [P, G, TB], F32R)
        ql = sb("ql", [P, G, TB])
        qs = sb("qs", [KS, J, G, TB], F32R)
        pt = sb("pt", [P, 4, TB])
        pw = sb("pw", [P, 2, HEADS * TB], F16)
        mid = sb("mid", [P, 2, TB], F32R)
        ks = sb("ks", [KS, J, G, N], F32R)
        kbd = sb("kbd", [P, G, J * N], F32R)
        vs = sb("vs", [N, HEADS, 3, VW], BF16)
        st1 = sb("st1", [P, TT, 6])
        mv1 = sb("mv1", [P, TT, 2])
        ln1 = sb("ln1", [P, 6, TT])
        st2 = ytmp[:, 0, 0:TT * 6].rearrange("p (t s) -> p t s", t=TT)
        mv2 = sb("mv2", [P, TT, 2])
        ln2 = sb("ln2", [P, 4, TT])
        rinv = sb("rinv", [P, 2, 2, HALF])
        mneg = ytmp[:, 1, 0:TT * HEADS].rearrange("p (t h) -> p t h", t=TT)
        msp = ytmp[:, 1, TT * HEADS:3 * TT * HEADS].rearrange("p (t h) -> p t h", t=TT)
        mrow = ytmp[0:2 * HEADS, 0, :]

        pair = [psum(f"pair{i}") for i in range(2)]
        sc = [psum(f"sc{i}") for i in range(2)]
        dv = [psum(f"dv{i}") for i in range(4)]

        k_dram = nc.dram_tensor("k_dram", (2, P, G, B, N), F32, kind="Internal").ap()
        v_dram = nc.dram_tensor("v_dram", (B, N, HEADS * 3 * VW), BF16, kind="Internal").ap()

        raw = pw[:, :, :].rearrange("p a f -> p (a f)").bitcast(F32)
        offset = [0]

        def stage(rows, cols, parts):
            a = raw[:, offset[0]:offset[0] + rows * cols].rearrange("p (c n) -> p c n", c=rows)
            offset[0] += rows * cols
            return a
        wq_raw = stage(DC, D, P)
        wk_raw = stage(LC, D, P)
        wv_raw = stage(LC, D, P)
        v2_raw = stage(1, D, P)
        u1_raw = stage(DC, RANK, P)
        u2_raw = stage(FC, RANK, P)
        v1_raw = x1[:, :, :].rearrange("p t d -> p (t d)")
        qflat = ql[:, :, :].rearrange("p g t -> p (g t)")
        c_raw = qflat[0:N, 0:B * L].rearrange("p (b l) -> p b l", b=B)
        c_nrm = qflat[0:N, B * L:2 * B * L].rearrange("p (b l) -> p b l", b=B)
        c_t = qflat[:, 2 * B * L:2 * B * L + LC * B * N].rearrange("p (c n) -> p c n", c=LC)
        kf = pt[:, 0, 0:B * N]
        k_hl = pt[:, 1, 0:2 * B * N].rearrange("p (i n) -> p i n", i=2)
        bv_all = pt[0:N, 2, :]
        ng, nb, tg, tb, bks = (pt[:, 3, 4 * i:4 * i + n] for i, n in enumerate((DC, DC, LC, LC, DC)))

        xa_in = sem("xa_in"); x1_in = sem("x1_in"); out_done = sem("out_done")
        ctx_in = sem("ctx_in"); vec_in = sem("vec_in"); row_in = sem("row_in")
        wq_in = sem("wq_in"); wkv_in = sem("wkv_in"); v1_in = sem("v1_in"); ffn_in = sem("ffn_in")
        k_saved = sem("k_saved"); v_saved = sem("v_saved")
        ks_in = sem("ks_in"); kbd_in = sem("kbd_in"); vs_in = sem("vs_in")
        q_in = sem("q_in"); m_in = sem("m_in")
        consts = sem("consts"); cleared = sem("cleared"); const_step = sem("const_step")
        setup_pe = sem("setup_pe"); setup_dve = sem("setup_dve"); setup_step = sem("setup_step")
        ctx_stats = sem("ctx_stats"); ctx_coef = sem("ctx_coef")
        w_hi = sem("w_hi"); w_lo = sem("w_lo"); wq_hi = sem("wq_hi"); wq_lo = sem("wq_lo")
        pair_full = sem("pair_full"); pair_hi = sem("pair_hi"); pair_lo = sem("pair_lo")
        sc_full = sem("sc_full"); sc_free = sem("sc_free")
        dv_full = sem("dv_full"); dv_free = sem("dv_free")
        exp_done = sem("exp_done"); ph_done = sem("ph_done")
        pl_even = sem("pl_even"); pl_odd = sem("pl_odd")
        st1_part = sem("st1_part"); st1_done = sem("st1_done"); ln1_step = sem("ln1_step")
        norm1 = sem("norm1")
        rinv_done = sem("rinv_done"); x1_sum = sem("x1_sum")
        st2_part = sem("st2_part"); st2_done = sem("st2_done"); ln2_step = sem("ln2_step")
        norm2 = sem("norm2"); x1_b2 = sem("x1_b2")
        gelu_done = sem("gelu_done"); h_hi = sem("h_hi"); h_even = sem("h_even"); h_odd = sem("h_odd")
        u2_done = sem("u2_done")
        m_red = sem("m_red"); m_hi = sem("m_hi"); m_lo = sem("m_lo"); m_row = sem("m_row")

        dve_waited = sem("dve_waited"); pool_waited = sem("pool_waited")

        LN1_STEPS, LN2_STEPS = 9, 4
        PROLOGUE_PAIR, PROLOGUE_DV = 3 * 4, TT * G + TT
        Q_DMAS, K_DMAS, KBD_DMAS = 3 * J, 3 * J, J

        class Turn:

            def __init__(self, k, has_next=True, has_x=True):
                self.k, self.has_next, self.has_x = k, has_next, has_x
                if has_next:
                    p0 = PROLOGUE_PAIR + 14 * k
                    self.q, self.t2, self.pu1, self.pu2, self.t1 = p0, p0 + 4, p0 + 8, p0 + 9, p0 + 10
                else:
                    p0 = PROLOGUE_PAIR + 14 * k - 4
                    self.q, self.t2, self.pu1, self.pu2, self.t1 = None, p0, p0 + 4, p0 + 5, None
                d0 = PROLOGUE_DV + 32 * k
                self.pv, self.sa, self.mt = d0, d0 + 8, d0 + 24
                self.v2 = d0 + 28 if has_next else d0 + 8
                self.sb, self.v1 = 32 * k, 32 * k + 16

        first = Turn(0)
        last_x = Turn(BLOCKS - 2, has_x=False)
        last = Turn(BLOCKS - 1, has_next=False, has_x=False)

        def run(eng, body):
            body(first)
            with eng.Fori(1, BLOCKS - 2) as k:
                body(Turn(k))
            body(last_x)
            body(last)

        T1_FIRST, Q_FIRST, T1_SECOND = 0, 4, 8

        block = stack.enter_context(nc.Block())

        @block.sync
        def _(sp):
            def tokens(ap, j):
                return ap[bass.ds(j * TB, TB), :].rearrange("(t p) d -> p t d", p=P)

            def load_keys(batch):
                for row, part in ((0, 0), (HD, 0), (2 * HD, 1)):
                    for j in range(J):
                        sp.dma_start(ks[row:row + HD, j].bitcast(F32),
                                     k_dram[part, HD * j:HD * (j + 1), :, bass.ds(batch, 1), :]
                                     .rearrange("d g b n -> d g (b n)")).then_inc(ks_in, DMA)

            def load_diagonal(batch):
                for j in range(J):
                    sp.dma_start(kbd[HD * j:HD * (j + 1), :, N * j:N * (j + 1)].bitcast(F32),
                                 k_dram[0, HD * j:HD * (j + 1), :, bass.ds(batch, 1), :]
                                 .rearrange("d g b n -> d g (b n)")).then_inc(kbd_in, DMA)

            def stack_q():
                for row, part in ((0, qh), (HD, ql), (2 * HD, qh)):
                    for j in range(J):
                        sp.dma_start(qs[row:row + HD, j].bitcast(F32),
                                     part[HD * j:HD * (j + 1)].bitcast(F32)).then_inc(q_in, DMA)

            def stack_max():
                for part in range(2):
                    sp.dma_start(qs[3 * HD + part:3 * HD + part + 1].bitcast(F32)
                                 .rearrange("p j g t -> p (j g) t"),
                                 mrow[HEADS * part:HEADS * (part + 1), :]).then_inc(m_in, DMA)

            sp.dma_start(xa[:], tokens(xf, 0)).then_inc(xa_in, DMA)
            sp.dma_start(c_raw, ctx.rearrange("b n l -> n b l")).then_inc(ctx_in, DMA)
            for dst, src in ((ng, norm_g), (nb, norm_b), (tg, tnorm_g), (tb, tnorm_b), (bqs[:], bq),
                             (bks, bk), (b1s[:], b1)):
                sp.dma_start(dst, src).then_inc(vec_in, DMA)
            sp.dma_start(wq_raw, Wq.rearrange("(c p) n -> p c n", p=P)).then_inc(wq_in, DMA)
            sp.dma_start(wk_raw, Wk.rearrange("(c p) n -> p c n", p=P)).then_inc(wkv_in, DMA)
            sp.dma_start(wv_raw, Wv.rearrange("(c p) n -> p c n", p=P)).then_inc(wkv_in, DMA)
            sp.dma_start(bv_all, bv.rearrange("(a d) -> a d", a=1).to_broadcast([N, D])).then_inc(row_in, DMA)
            sp.dma_start(b2_all[:], b2.rearrange("(a d) -> a d", a=1).to_broadcast([P, D])).then_inc(row_in, DMA)
            sp.dma_start(u1_raw, U1.rearrange("(c p) n -> p c n", p=P)).then_inc(ffn_in, DMA)
            sp.dma_start(v2_raw[:, 0, :], V2).then_inc(ffn_in, DMA)
            sp.dma_start(u2_raw, U2.rearrange("(c p) n -> p c n", p=P)).then_inc(ffn_in, DMA)
            sp.dma_start(v1_raw, V1).then_inc(v1_in, DMA)
            for g in range(G):
                sp.wait_ge(setup_dve, LC + 1 + g + 1)
                for part in range(2):
                    sp.dma_start(k_dram[part, :, g].rearrange("p b n -> p (b n)"),
                                 k_hl[:, part, :]).then_inc(k_saved, DMA)
            for n, b in enumerate(reversed(range(B))):
                sp.wait_ge(setup_dve, LC + 1 + G + n + 1)
                sp.dma_start(v_dram[b], vs[:].rearrange("n h i w -> n (h i w)")).then_inc(v_saved, DMA)
            sp.wait_ge(k_saved, DMA * 2 * G)
            sp.wait_ge(cleared, 2)
            load_diagonal(0)
            load_keys(0)
            sp.wait_ge(norm1, TT)
            sp.dma_start(xa[:], tokens(xf, 1)).then_inc(xa_in, DMA)
            sp.wait_ge(pair_lo, Q_FIRST + G)
            stack_q()
            sp.wait_ge(m_row, 1)
            stack_max()

            def body(t):
                k = t.k
                if t is first:
                    sp.wait_ge(w_lo, 4)
                at_least(sp, out_done, DMA * k)
                sp.dma_start(x1[:], tokens(xf, k)).then_inc(x1_in, DMA)
                if t is not first:
                    sp.wait_ge(dv_full, t.pv)
                    sp.dma_start(vs[:].rearrange("n h i w -> n (h i w)"),
                                 v_dram[bass.ds(k // PER_B, 1)].rearrange("b n f -> (b n) f")
                                 ).then_inc(vs_in, DMA)
                else:
                    sp.wait_ge(v_saved, DMA * B)
                if t.has_x:
                    sp.wait_ge(norm1, TT * (k + 2))
                    sp.dma_start(xa[:], tokens(xf, k + 2)).then_inc(xa_in, DMA)
                if t.has_next:
                    sp.wait_ge(dv_full, t.pv)
                    load_diagonal((k + 1) // PER_B)
                    sp.wait_ge(sc_full, t.sb + HEADS)
                    load_keys((k + 1) // PER_B)
                    sp.wait_ge(pair_lo, t.q + G)
                    stack_q()
                    sp.wait_ge(m_row, k + 2)
                    stack_max()
                sp.wait_ge(dv_free, t.v2 + TT)
                sp.dma_start(tokens(of, k), x1[:]).then_inc(out_done, DMA)

            run(sp, body)
            sp.wait_ge(out_done, DMA * BLOCKS)

        @block.tensor
        def _(pe):
            def three(o, w, m, first_pass, last_pass, names=None):
                pe.matmul(o, w(0), m(0), start=first_pass, stop=False)
                pe.matmul(o, w(0), m(1), start=False, stop=False)
                return pe.matmul(o, w(1), m(0), start=False, stop=last_pass)

            def pair_bank(use, u):
                at_least(pe, pair_lo, use - 1)
                return pair[u % 2]

            def dv_bank(use, u):
                at_least(pe, dv_free, use - 3)
                return dv[u % 4]

            def sc_bank(use, u):
                at_least(pe, sc_free, use - 1)
                return sc[u % 2]

            def turn_x(use):
                for c in range(DC):
                    bank = pair_bank(use + c, c)
                    for tt in range(TT):
                        mm = pe.transpose(bank[:, P * tt:P * (tt + 1)], xn[:, tt, P * c:P * (c + 1)], ident[:])
                    mm.then_inc(pair_full, 1)

            def project_q(use, g, between=None):
                bank = pair_bank(use + g, g)
                for c in range(DC):
                    mm = three(bank[:], lambda i: wq[:, i, c, P * g:P * (g + 1)],
                               lambda i: xt[:, i, c, :], c == 0, c == DC - 1)
                    if c == DC - 1:
                        mm.then_inc(pair_full, 1)
                    if between:
                        between(c)

            def max_pass(use, s):
                tt, g = divmod(s, G)
                bank = dv_bank(use + s, s)
                pe.matmul(bank[:, 0:J * N], qh[:, g, P * tt:P * (tt + 1)], kbd[:, g, :],
                          start=True, stop=True).then_inc(dv_full, 1)

            def turn_max(use, blk):
                pe.wait_ge(m_lo, blk + 1)
                at_least(pe, dv_free, use - 3)
                for tt in range(TT):
                    mm = pe.transpose(dv[0][0:2 * HEADS, P * tt:P * (tt + 1)], msp[:, tt, :], ident[:])
                mm.then_inc(dv_full, TT)

            def scores(t, g, j):
                h = J * g + j
                bank = sc_bank(t.sb + h, h)
                if h == 0:
                    pe.wait_ge(q_in, DMA * Q_DMAS * (t.k + 1))
                    pe.wait_ge(m_in, DMA * 2 * (t.k + 1))
                    pe.wait_ge(ks_in, DMA * K_DMAS * (t.k + 1))
                pe.matmul(bank[0:N, :], ks[:, j, g, :], qs[:, j, g, :],
                          start=True, stop=True).then_inc(sc_full, 1)

            pe.wait_ge(consts, 1)
            pe.wait_ge(setup_step, 1)
            for c in range(LC):
                for b in range(B):
                    mm = pe.transpose(dv[c][:, N * b:N * (b + 1)], c_nrm[:, b, P * c:P * (c + 1)], ident[0:N, 0:N])
                mm.then_inc(setup_pe, 1)
            pe.wait_ge(wq_in, DMA)
            pe.wait_ge(vec_in, DMA * 7)
            for g in range(G):
                for c in range(DC):
                    mm = pe.matmul(dv[3][:, g:g + 1], wq_raw[:, c, P * g:P * (g + 1)], nb[:, c:c + 1],
                                   start=(c == 0), stop=(c == DC - 1))
            mm.then_inc(setup_pe, 1)
            pe.wait_ge(wkv_in, DMA * 2)
            pe.wait_ge(setup_dve, LC)
            for g in range(G):
                for c in range(LC):
                    mm = pe.matmul((pair + sc)[g][:, 0:B * N], wk_raw[:, c, P * g:P * (g + 1)], c_t[:, c, :],
                                   start=(c == 0), stop=(c == LC - 1))
                mm.then_inc(setup_pe, 1)
            for n, b in enumerate(reversed(range(B))):
                for c in range(LC):
                    mm = pe.matmul(dv[n][0:N, :], c_t[:, c, N * b:N * (b + 1)], wv_raw[:, c, :],
                                   start=(c == 0), stop=(c == LC - 1))
                mm.then_inc(setup_pe, 1)

            pe.wait_ge(norm1, TT)
            pe.wait_ge(setup_dve, LC + 1 + 2)
            turn_x(T1_FIRST)
            pe.wait_ge(pair_lo, T1_FIRST + DC)
            pe.wait_ge(wq_lo, 1)
            for g in range(G):
                project_q(Q_FIRST, g)
            pe.wait_ge(pair_hi, Q_FIRST + G)
            pe.wait_ge(kbd_in, DMA * KBD_DMAS)
            pe.wait_ge(setup_dve, LC + 1 + G + B)
            for s in range(TT * G):
                max_pass(0, s)
            pe.wait_ge(norm1, TT * 2)
            turn_x(T1_SECOND)
            turn_max(TT * G, 0)

            def body(t):
                k = t.k
                if t.has_next:
                    pe.wait_ge(pair_lo, t.q)
                    for g in range(G):
                        project_q(t.q, g, lambda j: scores(t, g, j))
                else:
                    for g in range(G):
                        for j in range(J):
                            scores(t, g, j)
                for tt in range(TT):
                    for half in range(2):
                        u = 2 * tt + half
                        bank = dv_bank(t.pv + u, u)
                        if t is not first and u == 0:
                            pe.wait_ge(vs_in, DMA * k)
                        for hh in range(HALF):
                            h = HALF * half + hh
                            if tt == 0:
                                pe.wait_ge(pl_odd if h % 2 else pl_even, HALF * k + h // 2 + 1)
                            o = bank[:, VW * hh:VW * (hh + 1)]
                            w = [pw[0:N, i, TB * h + P * tt:TB * h + P * (tt + 1)] for i in range(2)]
                            terms = [(0, 0), (0, 1), (0, 2), (1, 0), (1, 1)]
                            for n, (i, v) in enumerate(terms):
                                mm = pe.matmul(o, w[i], vs[:, h, v, :], start=(n == 0), stop=(n == len(terms) - 1))
                        mm.then_inc(dv_full, 1)
                pe.wait_ge(norm2, TT * (k + 1))
                turn_x(t.t2)
                pe.wait_ge(pair_lo, t.t2 + DC)
                if t is first:
                    pe.wait_ge(w_lo, 4)
                bank = pair_bank(t.pu1, 0)
                for c in range(DC):
                    mm = three(bank[:], lambda i: u1[:, i, c, :], lambda i: xt[:, i, c, :], c == 0, c == DC - 1)
                mm.then_inc(pair_full, 1)
                pe.wait_ge(pair_lo, t.pu1 + 1)
                if t.has_next:
                    pe.wait_ge(pair_hi, t.q + G)
                    pe.wait_ge(kbd_in, DMA * KBD_DMAS * (k + 2))
                for s in range(FC + LAG):
                    if s < FC:
                        bank = sc_bank(t.v1 + s, s)
                        three(bank[:], lambda i: v1[:, i, P * s:P * (s + 1)], lambda i: mid[:, i, :],
                              True, True).then_inc(sc_full, 1)
                        if t.has_next:
                            max_pass(t.sa, s)
                    if s >= LAG:
                        f = s - LAG
                        if f == 0:
                            acc = pair_bank(t.pu2, 1)
                        pe.wait_ge(h_odd if f % 2 else h_even, FC // 2 * k + f // 2 + 1)
                        mm = three(acc[:], lambda i: u2[:, i, f, :], lambda i: xt[:, i, f % 4, :],
                                   f == 0, f == FC - 1)
                        mm.then_inc(u2_done, 1)
                pe.wait_ge(u2_done, FC * (k + 1))
                pe.nop().then_inc(pair_full, 1)
                if t.has_next:
                    turn_max(t.mt, k + 1)
                if t.has_x:
                    pe.wait_ge(norm1, TT * (k + 3))
                    turn_x(t.t1)
                pe.wait_ge(pair_lo, t.pu2 + 1)
                for tt in range(TT):
                    bank = dv_bank(t.v2 + tt, tt)
                    three(bank[:], lambda i: mid[:, i, P * tt:P * (tt + 1)], lambda i: v2[:, i, :],
                          True, True).then_inc(dv_full, 1)

            run(pe, body)

        @block.scalar
        def _(act):
            def high(use, u, o, bias=None):
                act.wait_ge(pair_full, use + 1)
                if bias is None:
                    act.activation(o, pair[u % 2][:], ACT.Copy).then_inc(pair_hi, 1)
                else:
                    act.activation(o, pair[u % 2][:], ACT.Identity, bias=bias).then_inc(pair_hi, 1)

            act.wait_ge(ffn_in, DMA * 3)
            act.copy(u1[:, 0], u1_raw).then_inc(w_hi, 1)
            act.copy(v2[:, 0], v2_raw[:, 0, :]).then_inc(w_hi, 1)
            act.copy(u2[:, 0], u2_raw).then_inc(w_hi, 1)
            act.wait_ge(v1_in, DMA)
            act.copy(v1[:, 0], v1_raw).then_inc(w_hi, 1)
            for c in range(DC):
                high(T1_FIRST + c, c, xt[:, 0, c, :])
            act.wait_ge(setup_dve, LC + 1)
            for g in range(G):
                high(Q_FIRST + g, g, qh[:, g, :], q_bias[:, g:g + 1])
            for c in range(DC):
                high(T1_SECOND + c, c, xt[:, 0, c, :])

            def body(t):
                k = t.k
                for g in range(G):
                    for j in range(J):
                        h = J * g + j
                        act.wait_ge(sc_full, t.sb + h + 1)
                        at_least(act, pl_odd if h % 2 else pl_even, HALF * k + (h - 4) // 2 + 1)
                        act.activation(pt[0:N, h % 4, :], sc[h % 2][0:N, :], ACT.Exp).then_inc(exp_done, 1)
                        act.wait_ge(exp_done, HEADS * k + h + 1)
                        act.nop().then_inc(sc_free, 1)
                    if t.has_next:
                        if g == 0:
                            act.wait_ge(q_in, DMA * Q_DMAS * (k + 1))
                        high(t.q + g, g, qh[:, g, :], q_bias[:, g:g + 1])
                act.wait_ge(ln2_step, LN2_STEPS * (k + 1))
                for tt in range(TT):
                    act.activation(xn[:, tt, :], x1[:, tt, :], ACT.Identity, bias=ln2[:, 3, tt:tt + 1],
                                   scale=ln2[:, 1, tt:tt + 1]).then_inc(norm2, 1)
                for c in range(DC):
                    high(t.t2 + c, c, xt[:, 0, c, :])
                high(t.pu1, 0, mid[:, 0, :])
                if t.has_next:
                    act.wait_ge(q_in, DMA * Q_DMAS * (k + 2))
                for f in range(FC):
                    act.wait_ge(sc_full, t.v1 + f + 1)
                    if f >= 4:
                        act.wait_ge(h_odd if f % 2 else h_even, FC // 2 * k + (f - 4) // 2 + 1)
                    act.activation(ql[:, f % 4, :], sc[f % 2][:], ACT.Gelu_apprx_tanh,
                                   bias=b1s[:, f:f + 1]).then_inc(gelu_done, 1)
                    act.wait_ge(gelu_done, FC * k + f + 1)
                    act.nop().then_inc(sc_free, 1)
                high(t.pu2, 1, mid[:, 0, :])
                if t.has_x:
                    for c in range(DC):
                        high(t.t1 + c, c, xt[:, 0, c, :])

            run(act, body)

        @block.vector
        def _(dve):
            def low(use, u, o, hi, bias=None):
                dve.wait_ge(pair_hi, use + 1)
                if bias is None:
                    dve.tensor_tensor(o, pair[u % 2][:], hi.bitcast(F32), ALU.subtract).then_inc(pair_lo, 1)
                else:
                    dve.scalar_tensor_tensor(out=o, in0=pair[u % 2][:], scalar=bias, in1=hi.bitcast(F32),
                                             op0=ALU.add, op1=ALU.subtract).then_inc(pair_lo, 1)

            def stats(src, st, mv, part, done, n):
                for tt in range(TT):
                    ins = dve.bn_stats(st[:, tt, :], src[:, tt, :])
                ins.then_inc(part, 1)
                dve.wait_ge(part, n + 1)
                dve.nop().then_inc(dve_waited, 1)
                for tt in range(TT):
                    ins = dve.bn_aggr(mv[:, tt, :], st[:, tt, :])
                ins.then_inc(done, 1)

            def reduce_max(use, s):
                tt, g = divmod(s, G)
                dve.wait_ge(dv_full, use + s + 1)
                o = mneg[:, tt, :].rearrange("p (j g) -> p j g", j=J)[:, :, g]
                dve.tensor_reduce(o, dv[s % 4][:, 0:J * N].rearrange("p (j n) -> p j n", j=J), AX.X, ALU.max,
                                  negate=True).then_inc(dv_free, 1)

            def split_max(blk, use):
                dve.wait_ge(dv_free, use)
                hi, lo = msp[:, :, 0:HEADS], msp[:, :, HEADS:2 * HEADS]
                dve.tensor_copy(hi.bitcast(F32R), mneg).then_inc(m_hi, 1)
                dve.wait_ge(m_hi, blk + 1)
                dve.tensor_tensor(lo.bitcast(F32R), mneg, hi, ALU.subtract).then_inc(m_lo, 1)

            def save_max(blk, use):
                at_least(dve, m_in, DMA * 2 * blk)
                dve.wait_ge(dv_full, use + TT)
                dve.tensor_copy(mrow, dv[0][0:2 * HEADS, :]).then_inc(m_row, 1)
                dve.wait_ge(m_row, blk + 1)
                dve.nop().then_inc(dv_free, TT)

            dve.wait_ge(xa_in, DMA)
            stats(xa, st1, mv1, st1_part, st1_done, 0)
            dve.wait_ge(ctx_in, DMA)
            for b in range(B):
                ins = dve.bn_stats(st2[0:N, b, :], c_raw[:, b, :])
            ins.then_inc(ctx_stats, 1)
            dve.wait_ge(ctx_stats, 1)
            for b in range(B):
                ins = dve.bn_aggr(mv2[0:N, b, :], st2[0:N, b, :])
            ins.then_inc(ctx_stats, 1)
            dve.wait_ge(ctx_coef, 2)
            for b in range(B):
                ins = dve.tensor_scalar(c_nrm[:, b, :], c_raw[:, b, :], mv2[0:N, b, 0:1], ln2[0:N, 1, b:b + 1],
                                        ALU.subtract, ALU.mult)
            ins.then_inc(setup_step, 1)
            dve.wait_ge(vec_in, DMA * 7)
            for c in range(LC):
                dve.wait_ge(setup_pe, c + 1)
                dve.tensor_scalar(c_t[:, c, :], dv[c][:, 0:B * N], tg[:, c:c + 1], tb[:, c:c + 1],
                                  ALU.mult, ALU.add).then_inc(setup_dve, 1)
            dve.wait_ge(setup_pe, LC + 1)
            dve.tensor_tensor(q_bias[:], dv[3][:, 0:DC], bqs[:], ALU.add).then_inc(setup_dve, 1)
            dve.wait_ge(wq_in, DMA)
            for c in range(DC):
                ins = dve.tensor_scalar(wq[:, 0, c, :], wq_raw[:, c, :], ng[:, c:c + 1], None, ALU.mult)
            ins.then_inc(wq_hi, 1)
            dve.wait_ge(wq_hi, 1)
            for c in range(DC):
                ins = dve.scalar_tensor_tensor(out=wq[:, 1, c, :], in0=wq_raw[:, c, :], scalar=ng[:, c:c + 1],
                                               in1=wq[:, 0, c, :].bitcast(F32), op0=ALU.mult, op1=ALU.subtract)
            ins.then_inc(wq_lo, 1)
            for g in range(G):
                dve.wait_ge(setup_pe, LC + 1 + g + 1)
                if g:
                    dve.wait_ge(k_saved, DMA * 2 * g)
                dve.tensor_scalar(kf, (pair + sc)[g][:, 0:B * N], bks[:, g:g + 1], SCALE,
                                  ALU.add, ALU.mult).then_inc(m_red, 1)
                dve.wait_ge(m_red, 2 * g + 1)
                dve.tensor_copy(k_hl[:, 0, :].bitcast(F32R), kf).then_inc(m_red, 1)
                dve.wait_ge(m_red, 2 * g + 2)
                dve.tensor_tensor(k_hl[:, 1, :].bitcast(F32R), kf, k_hl[:, 0, :],
                                  ALU.subtract).then_inc(setup_dve, 1)
            dve.wait_ge(row_in, DMA * 2)
            dve.wait_ge(cleared, 3)
            step = 2 * G
            for n, b in enumerate(reversed(range(B))):
                vf = ytmp[0:N, 1, :].rearrange("n (h d) -> n h d", h=HEADS)
                if n:
                    dve.wait_ge(v_saved, DMA * n)
                dve.wait_ge(setup_pe, LC + 1 + G + n + 1)
                dve.tensor_tensor(ytmp[0:N, 1, :], dv[n][0:N, :], bv_all, ALU.add).then_inc(m_red, 1)
                step += 1
                dve.wait_ge(m_red, step)
                for i in range(3):
                    part = vs[:, :, i, 0:HD]
                    dve.tensor_copy(part, vf).then_inc(m_red, 1)
                    step += 1
                    dve.wait_ge(m_red, step)
                    if i < 2:
                        dve.tensor_tensor(vf, vf, part, ALU.subtract).then_inc(m_red, 1)
                        step += 1
                        dve.wait_ge(m_red, step)
                dve.nop().then_inc(setup_dve, 1)

            for c in range(DC):
                low(T1_FIRST + c, c, xt[:, 1, c, :], xt[:, 0, c, :])
            for g in range(G):
                low(Q_FIRST + g, g, ql[:, g, :].bitcast(F32R), qh[:, g, :], q_bias[:, g:g + 1])
            dve.wait_ge(xa_in, DMA * 2)
            dve.wait_ge(norm1, TT)
            stats(xa, st1, mv1, st1_part, st1_done, 1)
            for s in range(TT * G):
                reduce_max(0, s)
            split_max(0, TT * G)
            for c in range(DC):
                low(T1_SECOND + c, c, xt[:, 1, c, :], xt[:, 0, c, :])
            save_max(0, TT * G)
            dve.wait_ge(w_lo, 4)

            def body(t):
                k = t.k
                for g in range(G):
                    for j in range(J):
                        h = J * g + j
                        dve.wait_ge(exp_done, HEADS * k + h + 1)
                        hi, lo = (pw[0:N, i, TB * h:TB * (h + 1)] for i in range(2))
                        dve.tensor_copy(hi, pt[0:N, h % 4, :]).then_inc(ph_done, 1)
                        if h % 2:
                            dve.wait_ge(ph_done, HEADS * k + h + 1)
                            dve.tensor_tensor(lo, pt[0:N, h % 4, :], hi, ALU.subtract).then_inc(pl_odd, 1)
                    if t.has_next:
                        low(t.q + g, g, ql[:, g, :].bitcast(F32R), qh[:, g, :], q_bias[:, g:g + 1])
                    if t.has_x and g == G - 2:
                        dve.wait_ge(xa_in, DMA * (k + 3))
                        dve.wait_ge(norm1, TT * (k + 2))
                        stats(xa, st1, mv1, st1_part, st1_done, k + 2)
                dve.wait_ge(x1_in, DMA * (k + 1))
                for tt in range(TT):
                    for half in range(2):
                        u = 2 * tt + half
                        bank = dv[u % 4][:, 0:HALF * VW].rearrange("p (h w) -> p h w", w=VW)
                        dve.wait_ge(dv_full, t.pv + u + 1)
                        dve.reciprocal(rinv[:, tt % 2, half, :], bank[:, :, HD]).then_inc(rinv_done, 1)
                        dve.wait_ge(rinv_done, 2 * TT * k + u + 1)
                        dve.tensor_tensor(
                            ytmp[:, tt % 2, 256 * half:256 * (half + 1)].rearrange("p (h d) -> p h d", d=HD),
                            bank[:, :, 0:HD],
                            rinv[:, tt % 2, half, :].unsqueeze(2).to_broadcast([P, HALF, HD]),
                            ALU.mult).then_inc(dv_free, 1)
                    dve.wait_ge(dv_free, t.pv + 2 * tt + 2)
                    dve.tensor_tensor(x1[:, tt, :], x1[:, tt, :], ytmp[:, tt % 2, :], ALU.add).then_inc(x1_sum, 1)
                dve.wait_ge(x1_sum, TT * (k + 1))
                stats(x1, st2, mv2, st2_part, st2_done, k)
                for c in range(DC):
                    low(t.t2 + c, c, xt[:, 1, c, :], xt[:, 0, c, :])
                low(t.pu1, 0, mid[:, 1, :], mid[:, 0, :])
                for f in range(FC):
                    dve.wait_ge(gelu_done, FC * k + f + 1)
                    if f >= 4:
                        dve.wait_ge(u2_done, FC * k + f - 3)
                    dve.tensor_copy(xt[:, 0, f % 4, :], ql[:, f % 4, :]).then_inc(h_hi, 1)
                    if t.has_next:
                        reduce_max(t.sa, f)
                    if f % 2 == 0:
                        dve.wait_ge(h_hi, FC * k + f + 1)
                        dve.tensor_tensor(xt[:, 1, f % 4, :], ql[:, f % 4, :], xt[:, 0, f % 4, :].bitcast(F32),
                                          ALU.subtract).then_inc(h_even, 1)
                if t.has_next:
                    split_max(k + 1, t.sa + TT * G)
                low(t.pu2, 1, mid[:, 1, :], mid[:, 0, :])
                if t.has_next:
                    save_max(k + 1, t.mt)
                if t.has_x:
                    for c in range(DC):
                        low(t.t1 + c, c, xt[:, 1, c, :], xt[:, 0, c, :])
                dve.wait_ge(x1_b2, TT * (k + 1))
                for tt in range(TT):
                    dve.wait_ge(dv_full, t.v2 + tt + 1)
                    dve.tensor_tensor(x1[:, tt, :], dv[tt % 4][:], x1[:, tt, :], ALU.add).then_inc(dv_free, 1)

            run(dve, body)

        @block.gpsimd
        def _(pool):
            def coefficients1(n):
                mean, var = mv1[:, :, 0], mv1[:, :, 1]
                s = LN1_STEPS * n
                pool.nop().then_inc(pool_waited, 1)
                pool.tensor_scalar(ln1[:, 0, :], var, EPS, 1.0, ALU.add, ALU.mult).then_inc(ln1_step, 1)
                pool.wait_ge(ln1_step, s + 1)
                pool.tensor_tensor(ln1[:, 1, :], ln1[:, 0, :], mhalf[:], ALU.pow).then_inc(ln1_step, 1)
                pool.wait_ge(ln1_step, s + 2)
                pool.tensor_tensor(ln1[:, 2, :], var, ln1[:, 1, :], ALU.mult).then_inc(ln1_step, 1)
                pool.wait_ge(ln1_step, s + 3)
                pool.tensor_tensor(ln1[:, 3, :], ln1[:, 2, :], ln1[:, 1, :], ALU.mult).then_inc(ln1_step, 1)
                pool.wait_ge(ln1_step, s + 4)
                pool.nop().then_inc(pool_waited, 1)
                pool.tensor_scalar(ln1[:, 0, :], ln1[:, 3, :], EPS, 1.0, ALU.add, ALU.mult).then_inc(ln1_step, 1)
                pool.wait_ge(ln1_step, s + 5)
                pool.tensor_tensor(ln1[:, 2, :], ln1[:, 0, :], mhalf[:], ALU.pow).then_inc(ln1_step, 1)
                pool.wait_ge(ln1_step, s + 6)
                pool.tensor_tensor(ln1[:, 4, :], ln1[:, 1, :], ln1[:, 2, :], ALU.mult).then_inc(ln1_step, 1)
                pool.wait_ge(ln1_step, s + 7)
                pool.tensor_tensor(ln1[:, 3, :], mean, ln1[:, 4, :], ALU.mult).then_inc(ln1_step, 1)
                pool.wait_ge(ln1_step, s + 8)
                pool.nop().then_inc(pool_waited, 1)
                pool.tensor_scalar(ln1[:, 5, :], ln1[:, 3, :], -1.0, 0.0, ALU.mult, ALU.add).then_inc(ln1_step, 1)
                pool.wait_ge(ln1_step, s + 9)

            def normalise(tt):
                pool.nop().then_inc(pool_waited, 1)
                pool.tensor_scalar(xn[:, tt, :], xa[:, tt, :], ln1[:, 4, tt:tt + 1], ln1[:, 5, tt:tt + 1],
                                   ALU.mult, ALU.add).then_inc(norm1, 1)

            pool.memset(mhalf[:], -0.5)
            pool.memset(ident[:], 0.0).then_inc(const_step, 1)
            pool.wait_ge(const_step, 1)
            pool.affine_select(out=ident[:], in_=ident[:], compare_op=ALU.not_equal, fill=1.0, base=0,
                               pattern=[[-1, P]], channel_multiplier=1).then_inc(consts, 1)
            pool.wait_ge(ctx_stats, 2)
            pool.tensor_scalar(ln2[0:N, 0, 0:B], mv2[0:N, 0:B, 1], EPS, 1.0, ALU.add, ALU.mult).then_inc(ctx_coef, 1)
            pool.wait_ge(ctx_coef, 1)
            pool.tensor_tensor(ln2[0:N, 1, 0:B], ln2[0:N, 0, 0:B], mhalf[0:N, 0:B], ALU.pow).then_inc(ctx_coef, 1)
            pool.wait_ge(st1_done, 1)
            coefficients1(0)
            for tt in range(TT):
                normalise(tt)
            pool.memset(kbd[:].bitcast(F32), 0.0).then_inc(cleared, 1)
            pool.wait_ge(cleared, 1)
            pool.memset(ks[3 * HD:KS].bitcast(F32), 1.0).then_inc(cleared, 1)
            pool.wait_ge(cleared, 2)
            pool.memset(vs[:, :, 0, HD:VW], 1.0)
            pool.memset(vs[:, :, 1:3, HD:VW], 0.0).then_inc(cleared, 1)
            for n, (w, w_raw) in enumerate(((u1, u1_raw), (v2, v2_raw[:, 0, :]), (u2, u2_raw), (v1, v1_raw))):
                pool.wait_ge(w_hi, n + 1)
                pool.tensor_tensor(w[:, 1], w_raw, w[:, 0].bitcast(F32), ALU.subtract).then_inc(w_lo, 1)
                if n == 1:
                    pool.wait_ge(st1_done, 2)
                    coefficients1(1)
                    pool.wait_ge(pair_full, T1_FIRST + DC)
                    for tt in range(TT):
                        normalise(tt)

            def body(t):
                k = t.k
                for h in range(0, HEADS, 2):
                    pool.wait_ge(ph_done, HEADS * k + h + 1)
                    hi, lo = (pw[0:N, i, TB * h:TB * (h + 1)] for i in range(2))
                    pool.tensor_tensor(lo, pt[0:N, h % 4, :], hi, ALU.subtract).then_inc(pl_even, 1)
                if t.has_x:
                    pool.wait_ge(st1_done, k + 3)
                    coefficients1(k + 2)
                pool.wait_ge(st2_done, k + 1)
                s = LN2_STEPS * k
                pool.nop().then_inc(pool_waited, 1)
                pool.tensor_scalar(ln2[:, 0, :], mv2[:, :, 1], EPS, 1.0, ALU.add, ALU.mult).then_inc(ln2_step, 1)
                pool.wait_ge(ln2_step, s + 1)
                pool.tensor_tensor(ln2[:, 1, :], ln2[:, 0, :], mhalf[:], ALU.pow).then_inc(ln2_step, 1)
                pool.wait_ge(ln2_step, s + 2)
                pool.tensor_tensor(ln2[:, 2, :], mv2[:, :, 0], ln2[:, 1, :], ALU.mult).then_inc(ln2_step, 1)
                pool.wait_ge(ln2_step, s + 3)
                pool.nop().then_inc(pool_waited, 1)
                pool.tensor_scalar(ln2[:, 3, :], ln2[:, 2, :], -1.0, 0.0, ALU.mult, ALU.add).then_inc(ln2_step, 1)
                pool.wait_ge(norm2, TT * (k + 1))
                chores = [("b2", tt) for tt in range(TT)] + ([("ln", tt) for tt in range(TT)] if t.has_x else [])
                for n in range(FC // 2):
                    f = 2 * n + 1
                    pool.wait_ge(h_hi, FC * k + f + 1)
                    pool.tensor_tensor(xt[:, 1, f % 4, :], ql[:, f % 4, :], xt[:, 0, f % 4, :].bitcast(F32),
                                       ALU.subtract).then_inc(h_odd, 1)
                    if n < len(chores):
                        what, tt = chores[n]
                        if what == "b2":
                            pool.tensor_tensor(x1[:, tt, :], x1[:, tt, :], b2_all[:], ALU.add).then_inc(x1_b2, 1)
                        else:
                            if tt == 0:
                                pool.wait_ge(pair_full, t.t2 + DC)
                            normalise(tt)

            run(pool, body)


_INS = ['x', 'ctx_768', 'L0_xattn_norm_g', 'L0_xattn_norm_b', 'L0_xattn_tnorm_g', 'L0_xattn_tnorm_b',
        'L0_xattn_Wq', 'L0_xattn_bq', 'L0_xattn_Wk', 'L0_xattn_bk', 'L0_xattn_Wv', 'L0_xattn_bv',
        'L0_ffn_U1', 'L0_ffn_V1', 'L0_ffn_b1', 'L0_ffn_U2', 'L0_ffn_V2', 'L0_ffn_b2']
_CHUNKED = {'L0_xattn_norm_g', 'L0_xattn_norm_b', 'L0_xattn_tnorm_g', 'L0_xattn_tnorm_b', 'L0_xattn_bq',
            'L0_xattn_bk', 'L0_ffn_b1'}


def kernel(**inputs):
    import numpy as _np
    import concourse.bacc as _bacc
    from concourse import mybir as _mybir
    from concourse.bass_utils import run_bass_kernel_spmd as _run

    nc = _bacc.Bacc("TRN2", target_bir_lowering=False, num_devices=1)
    arrays, args = {}, []
    for name in _INS:
        a = _np.asarray(inputs[name])
        if name in _CHUNKED:
            a = a.reshape(-1, 128).T
        a = _np.ascontiguousarray(a)
        arrays[f"in_{name}"] = a
        args.append(nc.dram_tensor(f"in_{name}", a.shape, _mybir.dt.from_np(a.dtype), kind="ExternalInput").ap())
    shape = _np.asarray(inputs['x']).shape
    args.append(nc.dram_tensor("out_0", shape, _mybir.dt.float32, kind="ExternalOutput").ap())
    xattn_ffn(nc, *args)
    r = _run(nc, [arrays], core_ids=[0])
    return r.results[0]["out_0"]
```

```python
from contextlib import ExitStack

import concourse.bass as bass
from concourse import mybir

ALU = mybir.AluOpType
ACT = mybir.ActivationFunctionType
AX = mybir.AxisListType
F32 = mybir.dt.float32
F32R = mybir.dt.float32r
F16 = mybir.dt.float16
BF16 = mybir.dt.bfloat16

P = 128
EPS = 1e-5
HEADS = 16
MAX_AHEAD = 4
LAG = 3
DMA = 16


def at_least(eng, sem, value):
    if isinstance(value, int) and value <= 0:
        return
    eng.wait_ge(sem, value)


def xattn_ffn(nc, x, ctx, norm_g, norm_b, tnorm_g, tnorm_b, Wq, bq, Wk, bk, Wv, bv,
              U1, V1, b1, U2, V2, b2, out):
    B, T, D = x.shape
    N, L = ctx.shape[1], ctx.shape[2]
    HD = D // HEADS
    RANK, F = V1.shape
    assert D == 512 and RANK == P and HD == 32
    DC, LC, FC = D // P, L // P, F // P
    TB = 512
    TT = TB // P
    BLOCKS = B * T // TB
    PER_B = T // TB
    G = HEADS // 4
    J = 4
    KS = 3 * HD + 2
    VW = HD + 1
    HALF = HEADS // 2
    SCALE = float(HD) ** -0.5

    xf = x.rearrange("b t d -> (b t) d")
    of = out.rearrange("b t d -> (b t) d")

    with ExitStack() as stack:
        def sb(name, shape, dt=F32):
            return stack.enter_context(nc.sbuf_tensor(name, shape, dt))

        def psum(name):
            return stack.enter_context(nc.psum_tensor(name, [P, 512], F32))

        def sem(name):
            return stack.enter_context(nc.semaphore(name))

        wq = sb("wq", [P, 2, DC, D], F32R)
        u1 = sb("u1", [P, 2, DC, RANK], F32R)
        v1 = sb("v1", [P, 2, F], F32R)
        u2 = sb("u2", [P, 2, FC, RANK], F32R)
        v2 = sb("v2", [P, 2, D], F32R)
        bqs = sb("bqs", [P, DC])
        b1s = sb("b1s", [P, FC])
        q_bias = sb("q_bias", [P, DC])
        b2_all = sb("b2_all", [P, D])
        ident = sb("ident", [P, P])
        mhalf = sb("mhalf", [P, 2 * TT])
        tables = mhalf[:, TT:TT + 1]
        x1 = sb("x1", [P, TT, D])
        xn = sb("xn", [P, TT, D])
        ytmp = sb("ytmp", [P, 2, D])
        y_half = [ytmp[:, tt // 2, D // 2 * (tt % 2):D // 2 * (tt % 2 + 1)] for tt in range(TT)]
        xt = sb("xt", [P, 2, DC, TB], F32R)
        x1t = sb("x1t", [P, 2, DC, TB], F32R)
        qh = sb("qh", [P, G, TB], F32R)
        ql = sb("ql", [P, G, TB])
        qs = sb("qs", [P, J, G, TB], F32R)
        pt = xn[0:N]
        pw = sb("pw", [P, 2, HEADS * TB], F16)
        mid = sb("mid", [P, 2, TB], F32R)
        ks = sb("ks", [KS, J, G, N], F32R)
        kbd = sb("kbd", [P, G, J * N], F32R)
        vs = sb("vs", [N, HEADS, 3, VW], BF16)
        mv1 = sb("mv1", [P, TT, 2])
        ln1 = sb("ln1", [P, 6, TT])
        st2 = sb("st2", [P, TT, 2, 6])
        st1 = st2[:, :, 1, :]
        mv2 = sb("mv2", [P, TT, 2])
        ln2 = sb("ln2", [P, 4, TT])
        rinv = sb("rinv", [P, 2, HALF])
        mneg = ytmp[:, 1, 0:TT * HEADS].rearrange("p (t h) -> p t h", t=TT)
        msp = ytmp[:, 1, TT * HEADS:3 * TT * HEADS].rearrange("p (t h) -> p t h", t=TT)
        mrow = ytmp[0:2 * HEADS, 0, :]

        pair = [psum(f"pair{i}") for i in range(2)]
        sc = [psum(f"sc{i}") for i in range(2)]
        dv = [psum(f"dv{i}") for i in range(4)]
        score_banks = [sc[0], pair[0], sc[1]]
        q_banks = [pair[1], pair[0], pair[1], dv[3]]
        hidden_banks = [sc[0], sc[1], pair[0]]
        t2_banks = [sc[0], sc[1], dv[0], dv[1]]
        t1_banks = [pair[0], sc[0], sc[1], pair[1]]

        k_dram = nc.dram_tensor("k_dram", (2, P, G, B, N), F32, kind="Internal").ap()
        v_dram = nc.dram_tensor("v_dram", (B, N, HEADS * 3 * VW), BF16, kind="Internal").ap()

        raw = pw[:, :, :].rearrange("p a f -> p (a f)").bitcast(F32)
        offset = [0]

        def stage(rows, cols, parts):
            a = raw[:, offset[0]:offset[0] + rows * cols].rearrange("p (c n) -> p c n", c=rows)
            offset[0] += rows * cols
            return a
        wq_raw = stage(DC, D, P)
        wk_raw = stage(LC, D, P)
        wv_raw = stage(LC, D, P)
        v2_raw = stage(1, D, P)
        u1_raw = stage(DC, RANK, P)
        u2_raw = stage(FC, RANK, P)
        v1_raw = x1[:, :, :].rearrange("p t d -> p (t d)")
        qflat = ql[:, :, :].rearrange("p g t -> p (g t)")
        c_raw = qflat[0:N, 0:B * L].rearrange("p (b l) -> p b l", b=B)
        c_nrm = qflat[0:N, B * L:2 * B * L].rearrange("p (b l) -> p b l", b=B)
        c_t = ytmp[:, 1, 0:LC * B * N].rearrange("p (c n) -> p c n", c=LC)
        other = raw[0:N, DC * D:DC * D + HEADS * 3 * VW // 2]
        v_other = other.bitcast(BF16).rearrange("n (h i w) -> n h i w", h=HEADS, i=3)
        vf = raw[0:N, DC * D + HEADS * 3 * VW // 2:DC * D + HEADS * 3 * VW // 2 + D]
        vecs = 2 * B * L
        ng, nb, tg, tb, bks = (qflat[:, vecs + 4 * i:vecs + 4 * i + n] for i, n in enumerate((DC, DC, LC, LC, DC)))
        kf = ytmp[:, 0, 0:B * N]
        k_hl = qs[:, 0:G, 0:2, 0:B * N]
        bv_all = b2_all[0:N, :]

        x_in = sem("x_in"); x1_in = sem("x1_in"); out_done = sem("out_done")
        ctx_in = sem("ctx_in"); kv_vec_in = sem("kv_vec_in"); vec_in = sem("vec_in"); row_in = sem("row_in")
        wq_in = sem("wq_in"); wk_in = sem("wk_in"); wv_in = sem("wv_in"); v1_in = sem("v1_in"); ffn_in = sem("ffn_in")
        k_saved = sem("k_saved"); v_saved = sem("v_saved"); v_other_saved = sem("v_other_saved")
        ks_in = sem("ks_in"); kbd_in = sem("kbd_in"); vs_in = sem("vs_in")
        q_in = sem("q_in"); ql_in = sem("ql_in"); ql_last_in = sem("ql_last_in"); m_in = sem("m_in")
        consts = sem("consts"); cleared = sem("cleared"); const_step = sem("const_step")
        setup_pe = sem("setup_pe"); setup_dve = sem("setup_dve"); setup_step = sem("setup_step")
        ctx_stats = sem("ctx_stats"); ctx_coef = sem("ctx_coef")
        w_hi = sem("w_hi"); w_lo = sem("w_lo"); u2_lo = sem("u2_lo"); wq_hi = sem("wq_hi"); wq_lo = sem("wq_lo")
        pair_full = sem("pair_full"); pair_hi = sem("pair_hi"); pair_lo = sem("pair_lo")
        sc_full = sem("sc_full"); sc_done = sem("sc_done")
        dv_full = sem("dv_full"); dv_free = sem("dv_free")
        ph_done = sem("ph_done")
        pl_even = sem("pl_even"); pl_odd = sem("pl_odd")
        st1_part = sem("st1_part"); st1_done = sem("st1_done"); ln1_step = sem("ln1_step")
        norm1 = sem("norm1")
        rinv_done = sem("rinv_done"); x1_half = sem("x1_half"); x1_sum = sem("x1_sum"); tables_in = sem("tables_in")
        st2_part = sem("st2_part"); st2_done = sem("st2_done"); ln2_step = sem("ln2_step")
        norm2_act = sem("norm2_act"); norm2_dve = sem("norm2_dve"); x1_b2 = sem("x1_b2")
        h_hi = sem("h_hi"); h_even = sem("h_even"); h_odd = sem("h_odd")
        u2_done = sem("u2_done")
        m_red = sem("m_red"); m_hi = sem("m_hi"); m_lo = sem("m_lo")

        dve_waited = sem("dve_waited"); pool_waited = sem("pool_waited")

        LN1_STEPS, LN2_STEPS = 9, 6
        PH = HEADS - HEADS // 4
        PROLOGUE_PAIR, PROLOGUE_DV = 3 * 4, TT * G + TT
        Q_DMAS, QL_DMAS, K_DMAS, KBD_DMAS = 4 * J, J, 3 * J, J
        Q_FIRST_DMAS = 2 * J

        class Turn:

            def __init__(self, k, has_next=True, has_x=True):
                self.k, self.has_next, self.has_x = k, has_next, has_x
                if has_next:
                    p0 = PROLOGUE_PAIR + 14 * k
                    self.q = [p0, p0 + 1, p0 + 2, p0 + 7]
                    self.t2, self.pu1 = p0 + 3, p0 + 8
                    self.pu2 = p0 + 10 if has_x else p0 + 9
                    self.t1 = [p0 + 9, p0 + 11, p0 + 12, p0 + 13]
                    self.x_use = p0 - DC
                else:
                    p0 = PROLOGUE_PAIR + 14 * k - 4
                    self.t2, self.pu1, self.pu2 = p0, p0 + 4, p0 + 5
                d0 = PROLOGUE_DV + 32 * k
                self.pv, self.sa, self.mt = d0, d0 + 8, d0 + 24
                self.v2 = d0 + 28 if has_next else d0 + 8
                self.sb, self.v1 = 32 * k, 32 * k + 16

                self.norm2 = TT // 2 * (k + 1)

        first = Turn(0)
        last_x = Turn(BLOCKS - 2, has_x=False)
        last = Turn(BLOCKS - 1, has_next=False, has_x=False)

        def run(eng, body):
            body(first)
            with eng.Fori(1, BLOCKS - 2) as k:
                body(Turn(k))
            body(last_x)
            body(last)

        T1_FIRST, Q_FIRST, T1_SECOND = 0, 4, 8

        block = stack.enter_context(nc.Block())

        @block.sync
        def _(sp):
            def tokens(ap, j):
                return ap[bass.ds(j * TB, TB), :].rearrange("(t p) d -> p t d", p=P)

            def load_keys(batch):
                for row, part in ((0, 0), (HD, 0), (2 * HD, 1)):
                    for j in range(J):
                        sp.dma_start(ks[row:row + HD, j].bitcast(F32),
                                     k_dram[part, HD * j:HD * (j + 1), :, bass.ds(batch, 1), :]
                                     .rearrange("d g b n -> d g (b n)")).then_inc(ks_in, DMA)

            def load_diagonal(batch):
                for j in range(J):
                    sp.dma_start(kbd[HD * j:HD * (j + 1), :, N * j:N * (j + 1)].bitcast(F32),
                                 k_dram[0, HD * j:HD * (j + 1), :, bass.ds(batch, 1), :]
                                 .rearrange("d g b n -> d g (b n)")).then_inc(kbd_in, DMA)

            def stack_q(a, b, low_in):
                for row, part, done in ((HD, ql, low_in), (0, qh, q_in), (2 * HD, qh, q_in)):
                    for j in range(J):
                        sp.dma_start(qs[row:row + HD, j, a:b].bitcast(F32),
                                     part[HD * j:HD * (j + 1), a:b].bitcast(F32)).then_inc(done, DMA)

            def stack_max():
                for part in range(2):
                    sp.dma_start(qs[3 * HD + part:3 * HD + part + 1].bitcast(F32)
                                 .rearrange("p j g t -> p (j g) t"),
                                 mrow[HEADS * part:HEADS * (part + 1), :]).then_inc(m_in, DMA)

            sp.dma_start(c_raw, ctx.rearrange("b n l -> n b l")).then_inc(ctx_in, DMA)
            for dst, src in ((tg, tnorm_g), (tb, tnorm_b), (bks, bk)):
                sp.dma_start(dst, src).then_inc(kv_vec_in, DMA)
            sp.dma_start(wk_raw, Wk.rearrange("(c p) n -> p c n", p=P)).then_inc(wk_in, DMA)
            sp.dma_start(xn[:], tokens(xf, 0)).then_inc(x_in, DMA)
            for dst, src in ((ng, norm_g), (nb, norm_b), (bqs[:], bq), (b1s[:], b1)):
                sp.dma_start(dst, src).then_inc(vec_in, DMA)
            sp.dma_start(wq_raw, Wq.rearrange("(c p) n -> p c n", p=P)).then_inc(wq_in, DMA)
            sp.dma_start(wv_raw, Wv.rearrange("(c p) n -> p c n", p=P)).then_inc(wv_in, DMA)
            sp.dma_start(bv_all, bv.rearrange("(a d) -> a d", a=1).to_broadcast([N, D])).then_inc(row_in, DMA)
            sp.dma_start(u1_raw, U1.rearrange("(c p) n -> p c n", p=P)).then_inc(ffn_in, DMA)
            sp.dma_start(v2_raw[:, 0, :], V2).then_inc(ffn_in, DMA)
            sp.dma_start(u2_raw, U2.rearrange("(c p) n -> p c n", p=P)).then_inc(ffn_in, DMA)
            sp.dma_start(v1_raw, V1).then_inc(v1_in, DMA)
            sp.wait_ge(setup_dve, LC + G)
            sp.wait_ge(cleared, 2)
            for j in range(J):
                sp.dma_start(kbd[HD * j:HD * (j + 1), :, N * j:N * (j + 1)].bitcast(F32),
                             k_hl[HD * j:HD * (j + 1), :, 0, 0:N].bitcast(F32)).then_inc(kbd_in, DMA)
            sp.wait_ge(pair_full, T1_FIRST + DC)
            sp.dma_start(xn[:], tokens(xf, 1)).then_inc(x_in, DMA)
            for row, part in ((0, 0), (HD, 0), (2 * HD, 1)):
                for j in range(J):
                    sp.dma_start(ks[row:row + HD, j].bitcast(F32),
                                 k_hl[HD * j:HD * (j + 1), :, part, 0:N].bitcast(F32)).then_inc(ks_in, DMA)
            for part in range(2):
                sp.dma_start(k_dram[part].rearrange("p g b n -> p g (b n)"),
                             k_hl[:, :, part, :].bitcast(F32)).then_inc(k_saved, DMA)
            sp.wait_ge(pair_lo, Q_FIRST + G)
            sp.wait_ge(kbd_in, DMA * KBD_DMAS)
            sp.wait_ge(ks_in, DMA * K_DMAS)
            sp.wait_ge(k_saved, DMA * 2)
            stack_q(0, G, ql_in)
            sp.wait_ge(setup_dve, LC + G + 1 + 1)
            sp.dma_start(v_dram[1], v_other.rearrange("n h i w -> n (h i w)")).then_inc(v_other_saved, DMA)
            sp.wait_ge(dv_free, PROLOGUE_DV)
            stack_max()
            sp.wait_ge(setup_dve, LC + G + 1 + B)
            sp.dma_start(v_dram[0], vs[:].rearrange("n h i w -> n (h i w)")).then_inc(v_saved, DMA)
            sp.dma_start(b2_all[:], b2.rearrange("(a d) -> a d", a=1).to_broadcast([P, D])).then_inc(row_in, DMA)

            def body(t):
                k = t.k
                if t is not first:
                    sp.wait_ge(out_done, DMA * k)
                else:
                    sp.wait_ge(v_saved, DMA)
                    sp.wait_ge(v_other_saved, DMA)
                    sp.wait_ge(w_lo, 3)
                sp.dma_start(x1[:], tokens(xf, k)).then_inc(x1_in, DMA)
                if t.has_next:
                    sp.wait_ge(dv_full, t.pv)
                    load_diagonal((k + 1) // PER_B)
                    sp.wait_ge(sc_full, t.sb + HEADS)
                    load_keys((k + 1) // PER_B)
                    sp.wait_ge(dv_full, t.pv + 2 * TT)
                    sp.dma_start(vs[:].rearrange("n h i w -> n (h i w)"),
                                 v_dram[bass.ds((k + 1) // PER_B, 1)].rearrange("b n f -> (b n) f")
                                 ).then_inc(vs_in, DMA)
                    sp.wait_ge(pair_lo, t.q[1] + 1)
                    stack_q(0, G // 2, ql_in)
                if t.has_x:
                    sp.wait_ge(pair_full, t.t2 + DC)
                    sp.dma_start(xn[:], tokens(xf, k + 2)).then_inc(x_in, DMA)
                if t.has_next:
                    sp.wait_ge(pair_lo, t.q[G - 1] + 1)
                    stack_q(G // 2, G, ql_last_in)
                    sp.wait_ge(dv_free, t.mt + TT)
                    stack_max()
                sp.wait_ge(dv_free, t.v2 + TT)
                sp.dma_start(tokens(of, k), x1[:]).then_inc(out_done, DMA)

            run(sp, body)
            sp.wait_ge(out_done, DMA * BLOCKS)

        @block.tensor
        def _(pe):
            def three(o, w, m, first_pass, last_pass, low_done=None, low_count=0):
                pe.matmul(o, w(0), m(0), start=first_pass, stop=False)
                pe.matmul(o, w(1), m(0), start=False, stop=False)
                if low_done is not None:
                    pe.wait_ge(low_done, low_count)
                return pe.matmul(o, w(0), m(1), start=False, stop=last_pass)

            def pair_bank(use, u):
                at_least(pe, pair_lo, use - 1)
                return pair[u % 2]

            def dv_bank(use, u):
                at_least(pe, dv_free, use - 3)
                return dv[u % 4]

            def turn_x(bank, c, tiles=range(TT)):
                for tt in tiles:
                    mm = pe.transpose(bank[:, P * tt:P * (tt + 1)], xn[:, tt, P * c:P * (c + 1)], ident[:])
                return mm

            def project_q(use, g, c, bank, x_use):
                if g == 0:
                    pe.wait_ge(pair_hi, x_use + c + 1)
                mm = three(bank[:], lambda i: wq[:, i, c, P * g:P * (g + 1)],
                           lambda i: xt[:, i, c, :], c == 0, c == DC - 1,
                           pair_lo if g == 0 else None, x_use + c + 1)
                if c == DC - 1:
                    mm.then_inc(pair_full, 1)

            def max_pass(use, s):
                g, tt = divmod(s, TT)
                bank = dv_bank(use + s, s)
                pe.matmul(bank[:, 0:J * N], qh[:, g, P * tt:P * (tt + 1)], kbd[:, g, :],
                          start=True, stop=True).then_inc(dv_full, 1)

            def turn_max(use, blk):
                pe.wait_ge(m_lo, blk + 1)
                at_least(pe, dv_free, use - 3)
                for tt in range(TT):
                    mm = pe.transpose(dv[0][0:2 * HEADS, P * tt:P * (tt + 1)], msp[:, tt, :], ident[:])
                mm.then_inc(dv_full, TT)

            def scores(t, h):
                g, j = divmod(h, J)
                if t.has_next and h < 3:
                    chunk = (None, 2, None)[h] if t is first else (1, 0, 2)[h]
                    if chunk is not None:
                        pe.wait_ge(pair_lo, t.x_use + chunk + 1)
                at_least(pe, sc_done, t.sb + h - 2)
                bank = score_banks[h % 3]
                if h == 0:
                    pe.wait_ge(q_in, DMA * (Q_DMAS * t.k + Q_FIRST_DMAS))
                    pe.wait_ge(ql_in, DMA * QL_DMAS * (t.k + 1))
                    at_least(pe, ql_last_in, DMA * QL_DMAS * t.k)
                    pe.wait_ge(m_in, DMA * 2 * (t.k + 1))
                    pe.wait_ge(ks_in, DMA * K_DMAS * (t.k + 1))
                pe.matmul(bank[0:N, :], ks[:, j, g, :], qs[0:KS, j, g, :],
                          start=True, stop=True).then_inc(sc_full, 1)

            def weights_values(t, half, tt, h):
                o = dv[tt][:, VW * (h - HALF * half):VW * (h - HALF * half + 1)]
                w = [pw[0:N, i, TB * h + P * tt:TB * h + P * (tt + 1)] for i in range(2)]
                terms = [(0, 0), (0, 1), (0, 2), (1, 0), (1, 1)]
                for n, (i, v) in enumerate(terms):
                    mm = pe.matmul(o, w[i], vs[:, h, v, :], start=(n == 0), stop=(n == len(terms) - 1))
                return mm

            def weights_ready(t, h):
                pe.wait_ge(pl_odd if h % 2 else pl_even, HALF * t.k + h // 2 + 1)

            def output_rows(t, tt):
                if t.has_next and tt == TT - 1:
                    pe.wait_ge(dv_free, t.mt + TT)
                bank = dv[(tt + 1) % TT]
                rows = slice(P * tt, P * (tt + 1))
                pe.matmul(bank[:], mid[:, 0, rows], v2[:, 0, :], start=True, stop=False)
                pe.matmul(bank[:], mid[:, 0, rows], v2[:, 1, :], start=False, stop=False)
                if tt == 0:
                    pe.wait_ge(pair_lo, t.pu2 + 1)
                pe.matmul(bank[:], mid[:, 1, rows], v2[:, 0, :], start=False, stop=True).then_inc(dv_full, 1)

            pe.wait_ge(consts, 1)
            pe.wait_ge(setup_step, 1)
            for c in range(LC):
                for b in range(B):
                    mm = pe.transpose(dv[c][:, N * b:N * (b + 1)], c_nrm[:, b, P * c:P * (c + 1)], ident[0:N, 0:N])
                mm.then_inc(setup_pe, 1)
            pe.wait_ge(wk_in, DMA)
            pe.wait_ge(setup_dve, LC)
            for g in range(G):
                for c in range(LC):
                    mm = pe.matmul((pair + sc)[g][:, 0:B * N], wk_raw[:, c, P * g:P * (g + 1)], c_t[:, c, :],
                                   start=(c == 0), stop=(c == LC - 1))
                mm.then_inc(setup_pe, 1)
            pe.wait_ge(wq_in, DMA)
            pe.wait_ge(vec_in, DMA * 4)
            for g in range(G):
                for c in range(DC):
                    mm = pe.matmul(dv[3][:, g:g + 1], wq_raw[:, c, P * g:P * (g + 1)], nb[:, c:c + 1],
                                   start=(c == 0), stop=(c == DC - 1))
            mm.then_inc(setup_pe, 1)

            pe.wait_ge(norm1, TT)
            pe.wait_ge(setup_dve, LC + 2)
            for c in range(DC):
                turn_x(pair_bank(T1_FIRST + c, c), c).then_inc(pair_full, 1)
            pe.wait_ge(wv_in, DMA)
            pe.wait_ge(setup_dve, LC + G)
            for b in reversed(range(B)):
                for c in range(LC):
                    mm = pe.matmul(sc[b][0:N, :], c_t[:, c, N * b:N * (b + 1)], wv_raw[:, c, :],
                                   start=(c == 0), stop=(c == LC - 1))
                mm.then_inc(setup_pe, 1)
            pe.wait_ge(wq_lo, 1)
            for g in range(G):
                for c in range(DC):
                    if c == 0:
                        pair_bank(Q_FIRST + g, g)
                    project_q(Q_FIRST + g, g, c, pair[g % 2], T1_FIRST)
            pe.wait_ge(pair_hi, Q_FIRST + G)
            pe.wait_ge(kbd_in, DMA * KBD_DMAS)
            for s in range(TT * G):
                max_pass(0, s)
            turn_max(TT * G, 0)
            pe.wait_ge(norm1, TT * 2)
            for c in range(DC):
                turn_x(pair_bank(T1_SECOND + c, c), c).then_inc(pair_full, 1)
            pe.wait_ge(w_lo, 2)
            pe.wait_ge(u2_lo, 1)
            pe.wait_ge(v_other_saved, DMA)
            pe.wait_ge(setup_dve, LC + G + 1 + B)

            def body(t):
                k = t.k
                for h in range(HEADS):
                    scores(t, h)
                    if h < HALF:
                        if t.has_next and h % 2:
                            if h == 1:
                                pe.wait_ge(pair_lo, t.x_use + DC)
                            project_q(t.q[0], 0, h // 2, q_banks[0], t.x_use)
                    else:
                        if h == HALF:
                            pe.wait_ge(dv_free, t.pv)
                            if t is not first:
                                pe.wait_ge(vs_in, DMA * k)
                        weights_ready(t, h - HALF)
                        for tt in range(TT):
                            mm = weights_values(t, 0, tt, h - HALF)
                            if h == HEADS - 1:
                                mm.then_inc(dv_full, 1)
                if t.has_next:
                    pe.wait_ge(sc_done, t.sb + HEADS - 2)
                    for c in range(DC):
                        project_q(t.q[1], 1, c, q_banks[1], t.x_use)
                for tt in range(TT):
                    for h in range(HALF, HEADS):
                        if tt == 0:
                            weights_ready(t, h)
                        if h == HALF:
                            pe.wait_ge(dv_free, t.pv + tt + 1)
                        mm = weights_values(t, 1, tt, h)
                    mm.then_inc(dv_full, 1)
                if t.has_next:
                    pe.wait_ge(pair_lo, t.q[0] + 1)
                    for c in range(DC):
                        project_q(t.q[2], 2, c, q_banks[2], t.x_use)
                    pe.wait_ge(dv_free, t.pv + 2 * TT)
                    for c in range(2):
                        project_q(t.q[3], 3, c, q_banks[3], t.x_use)
                pe.wait_ge(sc_done, t.sb + HEADS)
                pe.wait_ge(dv_free, t.pv + TT + 2)
                pe.wait_ge(norm2_act, t.norm2)
                for c in range(DC):
                    turn_x(t2_banks[c], c, range(0, TT // 2))
                if t.has_next:
                    project_q(t.q[3], 3, 2, q_banks[3], t.x_use)
                pe.wait_ge(norm2_dve, t.norm2)
                for c in range(DC):
                    turn_x(t2_banks[c], c, range(TT // 2, TT)).then_inc(pair_full, 1)
                if t.has_next:
                    project_q(t.q[3], 3, 3, q_banks[3], t.x_use)
                if t is first:
                    pe.wait_ge(w_lo, 3)
                if t.has_next:
                    pe.wait_ge(pair_lo, t.q[1] + 1)
                for c in range(DC):
                    pe.wait_ge(pair_hi, t.t2 + c + 1)
                    mm = three(pair[0][:], lambda i: u1[:, i, c, :], lambda i: x1t[:, i, c, :], c == 0, c == DC - 1,
                               pair_lo, t.t2 + c + 1)
                mm.then_inc(pair_full, 1)
                if t.has_next:
                    pe.wait_ge(kbd_in, DMA * KBD_DMAS * (k + 2))
                    for s in range(MAX_AHEAD):
                        if s == 2:
                            pe.wait_ge(pair_lo, t.q[G - 1] + 1)
                        max_pass(t.sa, s)
                pe.wait_ge(pair_hi, t.pu1 + 1)
                for s in range(FC + LAG):
                    if s < FC:
                        if s >= 3:
                            pe.wait_ge(sc_done, t.v1 + s - 2)
                        three(hidden_banks[s % 3][:], lambda i: v1[:, i, P * s:P * (s + 1)], lambda i: mid[:, i, :],
                              True, True, pair_lo if s == 0 else None, t.pu1 + 1).then_inc(sc_full, 1)
                        if t.has_next and s + MAX_AHEAD < TT * G:
                            if s + MAX_AHEAD == (G - 1) * TT:
                                pe.wait_ge(pair_hi, t.q[G - 1] + 1)
                            max_pass(t.sa, s + MAX_AHEAD)
                    if t.has_next and s == FC:
                        turn_max(t.mt, k + 1)
                    if s >= LAG:
                        f = s - LAG
                        if f == 0:
                            acc = pair[1]
                        if f % 2:
                            pe.wait_ge(h_hi, FC // 2 * k + f // 2 + 1)
                        else:
                            pe.wait_ge(sc_done, t.v1 + f + 1)
                        mm = three(acc[:], lambda i: u2[:, i, f, :], lambda i: x1t[:, i, f % 4, :],
                                   f == 0, f == FC - 1,
                                   h_odd if f % 2 else h_even, FC // 2 * k + f // 2 + 1)
                        mm.then_inc(u2_done if f < FC - 1 else pair_full, 1)
                    if t.has_x and s == FC + LAG - 2:
                        pe.wait_ge(norm1, TT * (k + 3))
                        pe.wait_ge(sc_done, t.v1 + FC - 1)
                        turn_x(t1_banks[0], 0).then_inc(pair_full, 1)
                if t.has_x:
                    for c in range(1, 3):
                        pe.wait_ge(sc_done, t.v1 + FC)
                        turn_x(t1_banks[c], c).then_inc(pair_full, 1)
                pe.wait_ge(pair_hi, t.pu2 + 1)
                for tt in range(TT):
                    output_rows(t, tt)
                    if t.has_x and tt == 0:
                        turn_x(t1_banks[DC - 1], DC - 1).then_inc(pair_full, 1)

            run(pe, body)

        @block.scalar
        def _(act):
            def high(use, bank, o, bias=None):
                act.wait_ge(pair_full, use + 1)
                if bias is None:
                    act.activation(o, bank[:], ACT.Copy).then_inc(pair_hi, 1)
                else:
                    act.activation(o, bank[:], ACT.Identity, bias=bias).then_inc(pair_hi, 1)

            def load_table(func, n):
                at_least(act, tables_in, n)
                act.activation(tables[:], mhalf[:, 0:1], func).then_inc(tables_in, 1)

            def normalise(tt):
                act.activation(xn[:, tt, :], xn[:, tt, :], ACT.Identity, bias=ln1[:, 5, tt:tt + 1],
                               scale=ln1[:, 4, tt:tt + 1]).then_inc(norm1, 1)

            act.wait_ge(wq_in, DMA)
            act.wait_ge(vec_in, DMA * 4)
            for c in range(DC):
                act.activation(wq[:, 0, c, :], wq_raw[:, c, :], ACT.Identity, scale=ng[:, c:c + 1]).then_inc(wq_hi, 1)
            act.wait_ge(ln1_step, LN1_STEPS)
            for tt in range(TT // 2, TT):
                normalise(tt)
            for c in range(DC):
                high(T1_FIRST + c, pair[c % 2], xt[:, 0, c, :])
            act.wait_ge(ffn_in, DMA * 3)
            act.copy(u1[:, 0], u1_raw).then_inc(w_hi, 1)
            act.copy(v2[:, 0], v2_raw[:, 0, :]).then_inc(w_hi, 1)
            act.wait_ge(setup_dve, LC + G + 1)
            for g in range(G):
                high(Q_FIRST + g, pair[g % 2], qh[:, g, :], q_bias[:, g:g + 1])
                if g == 0:
                    act.copy(u2[:, 0], u2_raw).then_inc(w_hi, 1)
                if g == 1:
                    act.wait_ge(v1_in, DMA)
                    act.copy(v1[:, 0], v1_raw).then_inc(w_hi, 1)
            act.wait_ge(ln1_step, LN1_STEPS * 2)
            for tt in range(TT // 2, TT):
                normalise(tt)
            for c in range(DC):
                high(T1_SECOND + c, pair[c % 2], xt[:, 0, c, :])
            load_table(ACT.Exp, 0)

            def body(t):
                k = t.k
                for h in range(HEADS):
                    act.wait_ge(sc_full, t.sb + h + 1)
                    at_least(act, pl_odd if h % 2 else pl_even, HALF * k + (h - 4) // 2 + 1)
                    ins = act.activation(pt[:, h % 4, :], score_banks[h % 3][0:N, :], ACT.Exp)
                    if h % 4 == 0:
                        ins = act.activation(pw[0:N, 0, TB * h:TB * (h + 1)], score_banks[h % 3][0:N, :], ACT.Exp)
                    ins.then_inc(sc_done, 1)
                    if t.has_next and h == 7:
                        act.wait_ge(q_in, DMA * (Q_DMAS * k + Q_FIRST_DMAS))
                        high(t.q[0], q_banks[0], qh[:, 0, :], q_bias[:, 0:1])
                load_table(ACT.Gelu_apprx_tanh, 2 * k + 1)
                if t.has_next:
                    high(t.q[1], q_banks[1], qh[:, 1, :], q_bias[:, 1:2])
                act.wait_ge(ln2_step, LN2_STEPS * k + 4)
                for tt in range(2):
                    act.activation(xn[:, tt, :], x1[:, tt, :], ACT.Identity, bias=ln2[:, 3, tt:tt + 1],
                                   scale=ln2[:, 1, tt:tt + 1]).then_inc(norm2_act, 1)
                if t.has_next:
                    high(t.q[2], q_banks[2], qh[:, 2, :], q_bias[:, 2:3])
                for c in range(DC):
                    high(t.t2 + c, t2_banks[c], x1t[:, 0, c, :])
                if t.has_next:
                    high(t.q[3], q_banks[3], qh[:, 3, :], q_bias[:, 3:4])
                high(t.pu1, pair[0], mid[:, 0, :])
                if t.has_next:
                    act.wait_ge(ql_in, DMA * QL_DMAS * (k + 2))
                for f in range(FC):
                    act.wait_ge(sc_full, t.v1 + f + 1)
                    if t.has_next and f == G // 2:
                        act.wait_ge(ql_last_in, DMA * QL_DMAS * (k + 1))
                    if f >= 4:
                        act.wait_ge(u2_done, (FC - 1) * k + f - 3)
                    ins = act.activation(ql[:, f % 4, :], hidden_banks[f % 3][:], ACT.Gelu_apprx_tanh,
                                         bias=b1s[:, f:f + 1])
                    if f % 2 == 0:
                        ins = act.activation(x1t[:, 0, f % 4, :], hidden_banks[f % 3][:], ACT.Gelu_apprx_tanh,
                                             bias=b1s[:, f:f + 1])
                    ins.then_inc(sc_done, 1)
                    if t.has_x and f >= FC - TT:
                        if f == FC - TT:
                            act.wait_ge(ln1_step, LN1_STEPS * (k + 3))
                        tt = f - (FC - TT)
                        normalise(tt)
                if t.has_x:
                    high(t.t1[0], t1_banks[0], xt[:, 0, 0, :])
                high(t.pu2, pair[1], mid[:, 0, :])
                if t.has_next:
                    load_table(ACT.Exp, 2 * k + 2)
                if t.has_x:
                    for c in range(1, DC):
                        high(t.t1[c], t1_banks[c], xt[:, 0, c, :])

            run(act, body)

        @block.vector
        def _(dve):
            def low(use, bank, o, hi, bias=None):
                dve.wait_ge(pair_hi, use + 1)
                if bias is None:
                    dve.tensor_tensor(o, bank[:], hi.bitcast(F32), ALU.subtract).then_inc(pair_lo, 1)
                else:
                    dve.scalar_tensor_tensor(out=o, in0=bank[:], scalar=bias, in1=hi.bitcast(F32),
                                             op0=ALU.add, op1=ALU.subtract).then_inc(pair_lo, 1)

            def stats(src, st, mv, part, done, n):
                for tt in range(TT):
                    ins = dve.bn_stats(st[:, tt, :], src[:, tt, :])
                ins.then_inc(part, 1)
                dve.wait_ge(part, n + 1)
                dve.nop().then_inc(dve_waited, 1)
                for tt in range(TT):
                    ins = dve.bn_aggr(mv[:, tt, :], st[:, tt, :])
                ins.then_inc(done, 1)

            def reduce_max(use, s):
                g, tt = divmod(s, TT)
                dve.wait_ge(dv_full, use + s + 1)
                o = mneg[:, tt, :].rearrange("p (j g) -> p j g", j=J)[:, :, g]
                dve.tensor_reduce(o, dv[s % 4][:, 0:J * N].rearrange("p (j n) -> p j n", j=J), AX.X, ALU.max,
                                  negate=True).then_inc(dv_free, 1)

            def split_max(blk, use):
                dve.wait_ge(dv_free, use)
                hi, lo = msp[:, :, 0:HEADS], msp[:, :, HEADS:2 * HEADS]
                dve.tensor_copy(hi.bitcast(F32R), mneg).then_inc(m_hi, 1)
                dve.wait_ge(m_hi, blk + 1)
                dve.tensor_tensor(lo.bitcast(F32R), mneg, hi, ALU.subtract).then_inc(m_lo, 1)

            def save_max(blk, use):
                at_least(dve, m_in, DMA * 2 * blk)
                dve.wait_ge(dv_full, use + TT)
                dve.tensor_copy(mrow, dv[0][0:2 * HEADS, :]).then_inc(dv_free, TT)

            dve.wait_ge(ctx_in, DMA)
            for b in range(B):
                ins = dve.bn_stats(st2[0:N, b, 0, :], c_raw[:, b, :])
            ins.then_inc(ctx_stats, 1)
            dve.wait_ge(ctx_stats, 1)
            for b in range(B):
                ins = dve.bn_aggr(mv2[0:N, b, :], st2[0:N, b, 0, :])
            ins.then_inc(ctx_stats, 1)
            dve.wait_ge(ctx_coef, 2)
            for b in range(B):
                ins = dve.tensor_scalar(c_nrm[:, b, :], c_raw[:, b, :], mv2[0:N, b, 0:1], ln2[0:N, 1, b:b + 1],
                                        ALU.subtract, ALU.mult)
            ins.then_inc(setup_step, 1)
            dve.wait_ge(kv_vec_in, DMA * 3)
            for c in range(LC):
                dve.wait_ge(setup_pe, c + 1)
                dve.tensor_scalar(c_t[:, c, :], dv[c][:, 0:B * N], tg[:, c:c + 1], tb[:, c:c + 1],
                                  ALU.mult, ALU.add).then_inc(setup_dve, 1)
            dve.wait_ge(x_in, DMA)
            stats(xn, st1, mv1, st1_part, st1_done, 0)
            for g in range(G):
                dve.wait_ge(setup_pe, LC + g + 1)
                dve.wait_ge(setup_dve, LC + g)
                dve.tensor_scalar(kf, (pair + sc)[g][:, 0:B * N], bks[:, g:g + 1], SCALE,
                                  ALU.add, ALU.mult).then_inc(m_red, 1)
                dve.wait_ge(m_red, 2 * g + 1)
                dve.tensor_copy(k_hl[:, g, 0, :], kf).then_inc(m_red, 1)
                dve.wait_ge(m_red, 2 * g + 2)
                dve.tensor_tensor(k_hl[:, g, 1, :], kf, k_hl[:, g, 0, :].bitcast(F32), ALU.subtract).then_inc(setup_dve, 1)
            for c in range(DC):
                dve.wait_ge(wq_hi, c + 1)
                ins = dve.scalar_tensor_tensor(out=wq[:, 1, c, :], in0=wq_raw[:, c, :], scalar=ng[:, c:c + 1],
                                               in1=wq[:, 0, c, :].bitcast(F32), op0=ALU.mult, op1=ALU.subtract)
            ins.then_inc(wq_lo, 1)
            dve.wait_ge(setup_pe, LC + G + 1)
            dve.tensor_tensor(q_bias[:], dv[3][:, 0:DC], bqs[:], ALU.add).then_inc(setup_dve, 1)
            def values(b):
                n = B - 1 - b
                step = 2 * G + 6 * n
                if n == 0:
                    dve.wait_ge(row_in, DMA)
                    dve.wait_ge(cleared, 3)
                dve.wait_ge(setup_pe, LC + G + 1 + n + 1)
                dve.tensor_tensor(vf, sc[b][0:N, :], bv_all, ALU.add).then_inc(m_red, 1)
                rest = vf.rearrange("n (h d) -> n h d", h=HEADS)
                for i in range(3):
                    part = (vs if b == 0 else v_other)[:, :, i, 0:HD]
                    dve.wait_ge(m_red, step + 2 * i + 1)
                    dve.tensor_copy(part, rest).then_inc(m_red, 1)
                    dve.wait_ge(m_red, step + 2 * i + 2)
                    if i < 2:
                        dve.tensor_tensor(rest, rest, part, ALU.subtract).then_inc(m_red, 1)
                dve.nop().then_inc(setup_dve, 1)

            for c in range(DC):
                low(T1_FIRST + c, pair[c % 2], xt[:, 1, c, :], xt[:, 0, c, :])
            for g in range(G):
                low(Q_FIRST + g, pair[g % 2], ql[:, g, :].bitcast(F32R), qh[:, g, :], q_bias[:, g:g + 1])
                if g == 0:
                    values(1)
                if g == 2:
                    dve.wait_ge(w_hi, 3)
                    dve.tensor_tensor(u2[:, 1], u2_raw, u2[:, 0].bitcast(F32), ALU.subtract).then_inc(u2_lo, 1)
            for s in range(TT * G):
                reduce_max(0, s)
            split_max(0, TT * G)
            dve.wait_ge(x_in, DMA * 2)
            stats(xn, st1, mv1, st1_part, st1_done, 1)
            save_max(0, TT * G)
            values(0)
            for c in range(DC):
                low(T1_SECOND + c, pair[c % 2], xt[:, 1, c, :], xt[:, 0, c, :])

            def output_rows(blk, use, tt):
                if tt == 0:
                    dve.wait_ge(x1_b2, TT * (blk + 1))
                dve.wait_ge(dv_full, use + tt + 1)
                dve.tensor_tensor(x1[:, tt, :], dv[(tt + 1) % TT][:], x1[:, tt, :], ALU.add).then_inc(dv_free, 1)

            def divide(t, half, tt):
                bank = dv[tt][:, 0:HALF * VW].rearrange("p (h w) -> p h w", w=VW)
                u = TT * half + tt
                dve.wait_ge(dv_full, t.pv + u + 1)
                dve.reciprocal(rinv[:, tt % 2, :], bank[:, :, HD]).then_inc(rinv_done, 1)
                dve.wait_ge(rinv_done, 2 * TT * t.k + u + 1)
                dve.tensor_tensor(y_half[tt].rearrange("p (h d) -> p h d", d=HD), bank[:, :, 0:HD],
                                  rinv[:, tt % 2, :].unsqueeze(2).to_broadcast([P, HALF, HD]),
                                  ALU.mult).then_inc(dv_free, 1)

            def body(t):
                k = t.k
                for h in range(HEADS):
                    if h % 4:
                        dve.wait_ge(sc_done, t.sb + h + 1)
                        hi, lo = (pw[0:N, i, TB * h:TB * (h + 1)] for i in range(2))
                        dve.tensor_copy(hi, pt[:, h % 4, :]).then_inc(ph_done, 1)
                        if h % 2:
                            dve.wait_ge(ph_done, PH * k + 3 * (h // 4) + h % 4)
                            dve.tensor_tensor(lo, pt[:, h % 4, :], hi, ALU.subtract).then_inc(pl_odd, 1)
                    if t.has_next and h == 9:
                        low(t.q[0], q_banks[0], ql[:, 0, :].bitcast(F32R), qh[:, 0, :], q_bias[:, 0:1])
                for tt in range(TT):
                    divide(t, 0, tt)
                for tt in range(TT + 1):
                    if tt < TT:
                        dve.wait_ge(x1_half, TT * k + tt + 1)
                        dve.bn_stats(st2[:, tt, 0, :], x1[:, tt, 0:D // 2])
                        divide(t, 1, tt)
                    elif t.has_next:
                        low(t.q[1], q_banks[1], ql[:, 1, :].bitcast(F32R), qh[:, 1, :], q_bias[:, 1:2])
                    if tt:
                        done = tt - 1
                        dve.wait_ge(x1_sum, TT * k + done + 1)
                        ins = dve.bn_stats(st2[:, done, 1, :], x1[:, done, D // 2:D])
                        if done % 2:
                            ins.then_inc(st2_part, 1)
                            dve.wait_ge(st2_part, 2 * k + done // 2 + 1)
                            dve.nop().then_inc(dve_waited, 1)
                            for i in (done - 1, done):
                                ins = dve.bn_aggr(mv2[:, i, :], st2[:, i, :, :])
                            ins.then_inc(st2_done, 1)
                dve.wait_ge(ln2_step, LN2_STEPS * (k + 1))
                for tt in range(TT // 2, TT):
                    dve.tensor_scalar(xn[:, tt, :], x1[:, tt, :], mv2[:, tt, 0:1], ln2[:, 1, tt:tt + 1],
                                      ALU.subtract, ALU.mult).then_inc(norm2_dve, 1)
                if t.has_next:
                    low(t.q[2], q_banks[2], ql[:, 2, :].bitcast(F32R), qh[:, 2, :], q_bias[:, 2:3])
                for c in range(DC):
                    low(t.t2 + c, t2_banks[c], x1t[:, 1, c, :], x1t[:, 0, c, :])
                if t.has_next:
                    low(t.q[3], q_banks[3], ql[:, 3, :].bitcast(F32R), qh[:, 3, :], q_bias[:, 3:4])
                low(t.pu1, pair[0], mid[:, 1, :], mid[:, 0, :])
                if t.has_next:
                    for s in range(MAX_AHEAD):
                        reduce_max(t.sa, s)
                for f in range(FC):
                    if f % 2:
                        dve.wait_ge(sc_done, t.v1 + f + 1)
                        if f >= 4:
                            dve.wait_ge(u2_done, (FC - 1) * k + f - 3)
                        dve.tensor_copy(x1t[:, 0, f % 4, :], ql[:, f % 4, :]).then_inc(h_hi, 1)
                    if t.has_next and f + MAX_AHEAD < TT * G:
                        reduce_max(t.sa, f + MAX_AHEAD)
                    if f % 2:
                        dve.wait_ge(h_hi, FC // 2 * k + f // 2 + 1)
                        dve.tensor_tensor(x1t[:, 1, f % 4, :], ql[:, f % 4, :], x1t[:, 0, f % 4, :].bitcast(F32),
                                          ALU.subtract).then_inc(h_odd, 1)
                    if t.has_next and f == TT * G - MAX_AHEAD:
                        split_max(k + 1, t.sa + TT * G)
                    if t.has_x:
                        if f == 1:
                            dve.wait_ge(x_in, DMA * (k + 3))
                        if 1 <= f < 1 + TT:
                            ins = dve.bn_stats(st1[:, f - 1, :], xn[:, f - 1, :])
                        if f == TT:
                            ins.then_inc(st1_part, 1)
                        if f == 1 + TT:
                            dve.wait_ge(st1_part, k + 3)
                            dve.nop().then_inc(dve_waited, 1)
                            for tt in range(TT):
                                ins = dve.bn_aggr(mv1[:, tt, :], st1[:, tt, :])
                            ins.then_inc(st1_done, 1)
                if t.has_next:
                    save_max(k + 1, t.mt)
                if t.has_x:
                    low(t.t1[0], t1_banks[0], xt[:, 1, 0, :], xt[:, 0, 0, :])
                low(t.pu2, pair[1], mid[:, 1, :], mid[:, 0, :])
                for tt in range(TT):
                    chunks = {0: (1, 2), 1: (3,)}.get(tt, ())
                    if t.has_x:
                        for c in chunks:
                            low(t.t1[c], t1_banks[c], xt[:, 1, c, :], xt[:, 0, c, :])
                    output_rows(k, t.v2, tt)

            run(dve, body)

        @block.gpsimd
        def _(pool):
            def coefficients1(n, part=None):
                mean, var = mv1[:, :, 0], mv1[:, :, 1]
                s = LN1_STEPS * n
                if part in (None, 0):
                    coefficients1_first(var, s)
                if part in (None, 1):
                    coefficients1_second(var, s)
                if part in (None, 2):
                    coefficients1_third(mean, s)

            def coefficients1_first(var, s):
                pool.nop().then_inc(pool_waited, 1)
                pool.tensor_scalar(ln1[:, 0, :], var, EPS, 1.0, ALU.add, ALU.mult).then_inc(ln1_step, 1)
                pool.wait_ge(ln1_step, s + 1)
                pool.tensor_tensor(ln1[:, 1, :], ln1[:, 0, :], mhalf[:, 0:TT], ALU.pow).then_inc(ln1_step, 1)

            def coefficients1_second(var, s):
                pool.wait_ge(ln1_step, s + 2)
                pool.tensor_tensor(ln1[:, 2, :], var, ln1[:, 1, :], ALU.mult).then_inc(ln1_step, 1)
                pool.wait_ge(ln1_step, s + 3)
                pool.tensor_tensor(ln1[:, 3, :], ln1[:, 2, :], ln1[:, 1, :], ALU.mult).then_inc(ln1_step, 1)
                pool.wait_ge(ln1_step, s + 4)
                pool.nop().then_inc(pool_waited, 1)
                pool.tensor_scalar(ln1[:, 0, :], ln1[:, 3, :], EPS, 1.0, ALU.add, ALU.mult).then_inc(ln1_step, 1)
                pool.wait_ge(ln1_step, s + 5)
                pool.tensor_tensor(ln1[:, 2, :], ln1[:, 0, :], mhalf[:, 0:TT], ALU.pow).then_inc(ln1_step, 1)

            def coefficients1_third(mean, s):
                pool.wait_ge(ln1_step, s + 6)
                pool.tensor_tensor(ln1[:, 4, :], ln1[:, 1, :], ln1[:, 2, :], ALU.mult).then_inc(ln1_step, 1)
                pool.wait_ge(ln1_step, s + 7)
                pool.tensor_tensor(ln1[:, 3, :], mean, ln1[:, 4, :], ALU.mult).then_inc(ln1_step, 1)
                pool.wait_ge(ln1_step, s + 8)
                pool.nop().then_inc(pool_waited, 1)
                pool.tensor_scalar(ln1[:, 5, :], ln1[:, 3, :], -1.0, 0.0, ALU.mult, ALU.add).then_inc(ln1_step, 1)
                pool.wait_ge(ln1_step, s + 9)

            def normalise(tt):
                pool.nop().then_inc(pool_waited, 1)
                pool.tensor_scalar(xn[:, tt, :], xn[:, tt, :], ln1[:, 4, tt:tt + 1], ln1[:, 5, tt:tt + 1],
                                   ALU.mult, ALU.add).then_inc(norm1, 1)

            def residual(t, half, tt):
                pool.wait_ge(dv_free, t.pv + TT * half + tt + 1)
                part = x1[:, tt, D // 2 * half:D // 2 * (half + 1)]
                pool.tensor_tensor(part, part, y_half[tt], ALU.add).then_inc(x1_sum if half else x1_half, 1)

            def coefficients2(t, half):
                a, b = 2 * half, 2 * half + 2
                s = LN2_STEPS * t.k + 4 * half
                pool.wait_ge(st2_done, 2 * t.k + half + 1)
                pool.nop().then_inc(pool_waited, 1)
                pool.tensor_scalar(ln2[:, 0, a:b], mv2[:, a:b, 1], EPS, 1.0, ALU.add, ALU.mult).then_inc(ln2_step, 1)
                pool.wait_ge(ln2_step, s + 1)
                pool.tensor_tensor(ln2[:, 1, a:b], ln2[:, 0, a:b], mhalf[:, a:b], ALU.pow).then_inc(ln2_step, 1)
                if half == 0:
                    pool.wait_ge(ln2_step, s + 2)
                    pool.tensor_tensor(ln2[:, 2, a:b], mv2[:, a:b, 0], ln2[:, 1, a:b], ALU.mult).then_inc(ln2_step, 1)
                    pool.wait_ge(ln2_step, s + 3)
                    pool.nop().then_inc(pool_waited, 1)
                    pool.tensor_scalar(ln2[:, 3, a:b], ln2[:, 2, a:b], -1.0, 0.0, ALU.mult,
                                       ALU.add).then_inc(ln2_step, 1)

            pool.memset(mhalf[:], -0.5)
            pool.memset(ident[:], 0.0).then_inc(const_step, 1)
            pool.wait_ge(const_step, 1)
            pool.affine_select(out=ident[:], in_=ident[:], compare_op=ALU.not_equal, fill=1.0, base=0,
                               pattern=[[-1, P]], channel_multiplier=1).then_inc(consts, 1)
            pool.memset(kbd[:].bitcast(F32), 0.0).then_inc(cleared, 1)
            pool.wait_ge(cleared, 1)
            pool.memset(ks[3 * HD:KS].bitcast(F32), 1.0).then_inc(cleared, 1)
            pool.wait_ge(ctx_stats, 2)
            pool.tensor_scalar(ln2[0:N, 0, 0:B], mv2[0:N, 0:B, 1], EPS, 1.0, ALU.add, ALU.mult).then_inc(ctx_coef, 1)
            pool.wait_ge(ctx_coef, 1)
            pool.tensor_tensor(ln2[0:N, 1, 0:B], ln2[0:N, 0, 0:B], mhalf[0:N, 0:B], ALU.pow).then_inc(ctx_coef, 1)
            pool.wait_ge(st1_done, 1)
            coefficients1(0)
            for tt in range(TT // 2):
                normalise(tt)
            pool.wait_ge(cleared, 2)
            pool.memset(vs[:, :, 0, HD:VW], 1.0)
            pool.wait_ge(setup_pe, LC + G)
            pool.memset(v_other[:, :, 0, HD:VW], 1.0)
            pool.memset(v_other[:, :, 1:3, HD:VW], 0.0)
            pool.memset(vs[:, :, 1:3, HD:VW], 0.0).then_inc(cleared, 1)
            for n, (w, w_raw) in enumerate(((u1, u1_raw), (v2, v2_raw[:, 0, :]))):
                pool.wait_ge(w_hi, n + 1)
                pool.tensor_tensor(w[:, 1], w_raw, w[:, 0].bitcast(F32), ALU.subtract).then_inc(w_lo, 1)
            pool.wait_ge(st1_done, 2)
            coefficients1(1)
            for tt in range(TT // 2):
                normalise(tt)
            pool.wait_ge(w_hi, 4)
            pool.tensor_tensor(v1[:, 1], v1_raw, v1[:, 0].bitcast(F32), ALU.subtract).then_inc(w_lo, 1)

            def body(t):
                k = t.k
                for h in range(0, HEADS, 2):
                    if h % 4:
                        pool.wait_ge(ph_done, PH * k + 3 * (h // 4) + h % 4)
                    else:
                        pool.wait_ge(sc_done, t.sb + h + 1)
                    hi, lo = (pw[0:N, i, TB * h:TB * (h + 1)] for i in range(2))
                    pool.tensor_tensor(lo, pt[:, h % 4, :], hi, ALU.subtract).then_inc(pl_even, 1)
                pool.wait_ge(x1_in, DMA * (k + 1))
                for tt in range(TT):
                    residual(t, 0, tt)
                for tt in range(TT):
                    residual(t, 1, tt)
                    if tt == TT // 2:
                        coefficients2(t, 0)
                coefficients2(t, 1)
                for n in range(FC // 2):
                    f = 2 * n
                    pool.wait_ge(sc_done, t.v1 + f + 1)
                    pool.tensor_tensor(x1t[:, 1, f % 4, :], ql[:, f % 4, :], x1t[:, 0, f % 4, :].bitcast(F32),
                                       ALU.subtract).then_inc(h_even, 1)
                    if n in (0, 1, 2, 5):
                        tt = min(n, TT - 1)
                        if n == 0:
                            pool.wait_ge(norm2_act, t.norm2)
                            pool.wait_ge(norm2_dve, t.norm2)
                            if t is first:
                                pool.wait_ge(row_in, DMA * 2)
                        pool.tensor_tensor(x1[:, tt, :], x1[:, tt, :], b2_all[:], ALU.add).then_inc(x1_b2, 1)
                    if 3 <= n < 6 and t.has_x:
                        if n == 3:
                            pool.wait_ge(st1_done, k + 3)
                        coefficients1(k + 2, n - 3)

            run(pool, body)


_INS = ['x', 'ctx_768', 'L0_xattn_norm_g', 'L0_xattn_norm_b', 'L0_xattn_tnorm_g', 'L0_xattn_tnorm_b',
        'L0_xattn_Wq', 'L0_xattn_bq', 'L0_xattn_Wk', 'L0_xattn_bk', 'L0_xattn_Wv', 'L0_xattn_bv',
        'L0_ffn_U1', 'L0_ffn_V1', 'L0_ffn_b1', 'L0_ffn_U2', 'L0_ffn_V2', 'L0_ffn_b2']
_CHUNKED = {'L0_xattn_norm_g', 'L0_xattn_norm_b', 'L0_xattn_tnorm_g', 'L0_xattn_tnorm_b', 'L0_xattn_bq',
            'L0_xattn_bk', 'L0_ffn_b1'}


def kernel(**inputs):
    import numpy as _np
    import concourse.bacc as _bacc
    from concourse import mybir as _mybir
    from concourse.bass_utils import run_bass_kernel_spmd as _run

    nc = _bacc.Bacc("TRN2", target_bir_lowering=False, num_devices=1)
    arrays, args = {}, []
    for name in _INS:
        a = _np.asarray(inputs[name])
        if name in _CHUNKED:
            a = a.reshape(-1, 128).T
        a = _np.ascontiguousarray(a)
        arrays[f"in_{name}"] = a
        args.append(nc.dram_tensor(f"in_{name}", a.shape, _mybir.dt.from_np(a.dtype), kind="ExternalInput").ap())
    shape = _np.asarray(inputs['x']).shape
    args.append(nc.dram_tensor("out_0", shape, _mybir.dt.float32, kind="ExternalOutput").ap())
    xattn_ffn(nc, *args)
    r = _run(nc, [arrays], core_ids=[0])
    return r.results[0]["out_0"]
```

```python
from contextlib import ExitStack

import concourse.bass as bass
from concourse import mybir

ALU = mybir.AluOpType
ACT = mybir.ActivationFunctionType
AX = mybir.AxisListType
F32 = mybir.dt.float32
F32R = mybir.dt.float32r
F16 = mybir.dt.float16
BF16 = mybir.dt.bfloat16

P = 128
EPS = 1e-5
HEADS = 16
MAX_AHEAD = 4
LAG = 3
DMA = 16


def at_least(eng, sem, value):
    if isinstance(value, int) and value <= 0:
        return
    eng.wait_ge(sem, value)


def xattn_ffn(nc, x, ctx, norm_g, norm_b, tnorm_g, tnorm_b, Wq, bq, Wk, bk, Wv, bv,
              U1, V1, b1, U2, V2, b2, out):
    B, T, D = x.shape
    N, L = ctx.shape[1], ctx.shape[2]
    HD = D // HEADS
    RANK, F = V1.shape
    assert D == 512 and RANK == P and HD == 32
    DC, LC, FC = D // P, L // P, F // P
    TB = 512
    TT = TB // P
    BLOCKS = B * T // TB
    PER_B = T // TB
    G = HEADS // 4
    J = 4
    KS = 3 * HD + 2
    VW = HD + 1
    HALF = HEADS // 2
    SCALE = float(HD) ** -0.5

    xf = x.rearrange("b t d -> (b t) d")
    of = out.rearrange("b t d -> (b t) d")

    with ExitStack() as stack:
        def sb(name, shape, dt=F32):
            return stack.enter_context(nc.sbuf_tensor(name, shape, dt))

        def psum(name):
            return stack.enter_context(nc.psum_tensor(name, [P, 512], F32))

        def sem(name):
            return stack.enter_context(nc.semaphore(name))

        wq = sb("wq", [P, 2, DC, D], F32R)
        u1 = sb("u1", [P, 2, DC, RANK], F32R)
        v1 = sb("v1", [P, 2, F], F32R)
        u2 = sb("u2", [P, 2, FC, RANK], F32R)
        v2 = sb("v2", [P, 2, D], F32R)
        bqs = sb("bqs", [P, DC])
        b1s = sb("b1s", [P, FC])
        q_bias = sb("q_bias", [P, DC])
        b2_all = sb("b2_all", [P, D])
        ident = sb("ident", [P, P])
        mhalf = sb("mhalf", [P, 2 * TT])
        tables = mhalf[:, TT:TT + 1]
        x1 = sb("x1", [P, TT, D])
        xn = sb("xn", [P, TT, D])
        ytmp = sb("ytmp", [P, 2, D])
        y_half = [ytmp[:, tt // 2, D // 2 * (tt % 2):D // 2 * (tt % 2 + 1)] for tt in range(TT)]
        xt = sb("xt", [P, 2, DC, TB], F32R)
        x1t = sb("x1t", [P, 2, DC, TB], F32R)
        qh = sb("qh", [P, G, TB], F32R)
        ql = sb("ql", [P, G, TB])
        qs = sb("qs", [P, J, G, TB], F32R)
        pt = xn[0:N]
        pw = sb("pw", [P, 2, HEADS * TB], F16)
        mid = sb("mid", [P, 2, TB], F32R)
        ks = sb("ks", [KS, J, G, N], F32R)
        kbd = sb("kbd", [P, G, J * N], F32R)
        vs = sb("vs", [N, HEADS, 3, VW], BF16)
        mv1 = sb("mv1", [P, TT, 2])
        ln1 = sb("ln1", [P, 6, TT])
        st2 = sb("st2", [P, TT, 2, 6])
        st1 = st2[:, :, 1, :]
        mv2 = sb("mv2", [P, TT, 2])
        ln2 = sb("ln2", [P, 4, TT])
        rinv = sb("rinv", [P, 2, HALF])
        mneg = ytmp[:, 1, 0:TT * HEADS].rearrange("p (t h) -> p t h", t=TT)
        msp = ytmp[:, 1, TT * HEADS:3 * TT * HEADS].rearrange("p (t h) -> p t h", t=TT)
        mrow = ytmp[0:2 * HEADS, 0, :]

        pair = [psum(f"pair{i}") for i in range(2)]
        sc = [psum(f"sc{i}") for i in range(2)]
        dv = [psum(f"dv{i}") for i in range(4)]
        key_banks = [dv[0], dv[1], dv[2], sc[0]]
        t1_second_banks = [pair[0], sc[1], pair[1], dv[2]]
        score_banks = [sc[0], pair[0], sc[1]]
        q_banks = [pair[1], pair[0], pair[1], dv[3]]
        hidden_banks = [sc[0], sc[1], pair[0]]
        t2_banks = [sc[0], sc[1], dv[0], dv[1]]
        t1_banks = [pair[0], sc[0], sc[1], pair[1]]

        k_dram = nc.dram_tensor("k_dram", (2, P, G, B, N), F32, kind="Internal").ap()
        v_dram = nc.dram_tensor("v_dram", (B, N, HEADS * 3 * VW), BF16, kind="Internal").ap()

        raw = pw[:, :, :].rearrange("p a f -> p (a f)").bitcast(F32)
        offset = [0]

        def stage(rows, cols):
            a = raw[:, offset[0]:offset[0] + rows * cols].rearrange("p (c n) -> p c n", c=rows)
            offset[0] += rows * cols
            return a
        wq_raw = stage(DC, D)
        wk_raw = stage(LC, D)
        wv_raw = stage(LC, D)
        c_t = stage(1, D)[:, 0, 0:LC * B * N].rearrange("p (c n) -> p c n", c=LC)
        u1_raw = stage(DC, RANK)
        u2_raw = stage(FC, RANK)
        v1_raw = x1[:, :, :].rearrange("p t d -> p (t d)")
        qflat = ql[:, :, :].rearrange("p g t -> p (g t)")
        c_raw = qflat[0:N, 0:B * L].rearrange("p (b l) -> p b l", b=B)
        c_nrm = qflat[0:N, B * L:2 * B * L].rearrange("p (b l) -> p b l", b=B)
        v2_raw = ytmp[:, 1, :]
        other = raw[0:N, 0:HEADS * 3 * VW // 2]
        v_other = other.bitcast(BF16).rearrange("n (h i w) -> n h i w", h=HEADS, i=3)
        vf_at = [(DC - 1) * D, (DC - 2) * D]
        vf = [raw[0:N, a:a + D] for a in vf_at]
        vecs = 2 * B * L
        ng, nb, tg, tb, bks = (qflat[:, vecs + 4 * i:vecs + 4 * i + n] for i, n in enumerate((DC, DC, LC, LC, DC)))
        kf = ytmp[:, 0, 0:B * N]
        bias_row = ytmp[0:1, 0, :]
        k_hl = raw[:, DC * D:DC * D + 2 * G * B * N].bitcast(F32R).rearrange("p (g i n) -> p g i n", g=G, i=2)
        bv_all = b2_all[0:N, :]

        x_in = sem("x_in"); x1_in = sem("x1_in"); out_done = sem("out_done")
        ctx_in = sem("ctx_in"); kv_vec_in = sem("kv_vec_in"); vec_in = sem("vec_in"); row_in = sem("row_in")
        wq_in = sem("wq_in"); wk_in = sem("wk_in"); wv_in = sem("wv_in"); v1_in = sem("v1_in"); ffn_in = sem("ffn_in")
        k_saved = sem("k_saved"); v_saved = sem("v_saved"); v_other_saved = sem("v_other_saved")
        ks_in = sem("ks_in"); kbd_in = sem("kbd_in"); vs_in = sem("vs_in")
        q_in = sem("q_in"); ql_in = sem("ql_in"); ql_last_in = sem("ql_last_in"); m_in = sem("m_in")
        consts = sem("consts"); cleared = sem("cleared"); const_step = sem("const_step"); row_out = sem("row_out")
        setup_pe = sem("setup_pe"); setup_dve = sem("setup_dve"); setup_step = sem("setup_step")
        ctx_stats = sem("ctx_stats"); ctx_coef = sem("ctx_coef")
        w_hi = sem("w_hi"); w_lo = sem("w_lo"); wq_hi = sem("wq_hi"); wq_lo = sem("wq_lo")
        pair_full = sem("pair_full"); pair_hi = sem("pair_hi"); pair_lo = sem("pair_lo")
        sc_full = sem("sc_full"); sc_done = sem("sc_done")
        dv_full = sem("dv_full"); dv_free = sem("dv_free")
        ph_done = sem("ph_done")
        pl_even = sem("pl_even"); pl_odd = sem("pl_odd")
        st1_part = sem("st1_part"); st1_done = sem("st1_done"); ln1_step = sem("ln1_step")
        norm1 = sem("norm1")
        rinv_done = sem("rinv_done"); x1_half = sem("x1_half"); x1_sum = sem("x1_sum"); tables_in = sem("tables_in")
        st2_part = sem("st2_part"); st2_done = sem("st2_done"); ln2_step = sem("ln2_step")
        norm2_act = sem("norm2_act"); norm2_dve = sem("norm2_dve"); x1_b2 = sem("x1_b2")
        h_hi = sem("h_hi"); h_even = sem("h_even"); h_odd = sem("h_odd")
        u2_done = sem("u2_done")
        m_red = sem("m_red"); m_hi = sem("m_hi"); m_lo = sem("m_lo")

        dve_waited = sem("dve_waited"); pool_waited = sem("pool_waited")

        LN1_STEPS, LN2_STEPS = 9, 6
        PH = HEADS - HEADS // 4
        PROLOGUE_PAIR, PROLOGUE_DV = 3 * 4, TT * G + TT
        FFN_WEIGHTS = 4
        Q_DMAS, QL_DMAS, K_DMAS, KBD_DMAS = 2 * J, J, 3 * J, J

        BIAS_DONE = LC + 1
        KEYS_DONE = BIAS_DONE + G

        class Turn:

            def __init__(self, k, batch, next_batch=None, has_next=True, has_x=True):
                self.batch, self.next_batch = batch, batch if next_batch is None else next_batch
                self.k, self.has_next, self.has_x = k, has_next, has_x
                if has_next:
                    p0 = PROLOGUE_PAIR + 14 * k
                    self.q = [p0, p0 + 1, p0 + 2, p0 + 7]
                    self.t2, self.pu1 = p0 + 3, p0 + 8
                    self.pu2 = p0 + 10 if has_x else p0 + 9
                    self.t1 = [p0 + 9, p0 + 11, p0 + 12, p0 + 13]
                    self.x_use = p0 - DC
                else:
                    p0 = PROLOGUE_PAIR + 14 * k - 4
                    self.t2, self.pu1, self.pu2 = p0, p0 + 4, p0 + 5
                d0 = PROLOGUE_DV + 32 * k
                self.pv, self.sa, self.mt = d0, d0 + 8, d0 + 24
                self.v2 = d0 + 28 if has_next else d0 + 8
                self.sb, self.v1 = 32 * k, 32 * k + 16
                self.norm2 = TT // 2 * (k + 1)

        first = Turn(0, 0)
        last_x = Turn(BLOCKS - 2, B - 1, has_x=False)
        last = Turn(BLOCKS - 1, B - 1, has_next=False, has_x=False)

        def run(eng, body):
            body(first)
            for b in range(B):
                start = 1 if b == 0 else b * PER_B
                end = (b + 1) * PER_B - 1 if b < B - 1 else BLOCKS - 2
                with eng.Fori(start, end) as k:
                    body(Turn(k, b))
                if b < B - 1:
                    body(Turn(end, b, b + 1))
            body(last_x)
            body(last)

        T1_FIRST, Q_FIRST, T1_SECOND = 0, 4, 8

        block = stack.enter_context(nc.Block())

        @block.sync
        def _(sp):
            def tokens(ap, j):
                return ap[bass.ds(j * TB, TB), :].rearrange("(t p) d -> p t d", p=P)

            def load_keys(batch):
                for row, part in ((0, 0), (HD, 0), (2 * HD, 1)):
                    for j in range(J):
                        sp.dma_start(ks[row:row + HD, j].bitcast(F32),
                                     k_dram[part, HD * j:HD * (j + 1), :, batch, :]).then_inc(ks_in, DMA)

            def load_diagonal(batch):
                for j in range(J):
                    sp.dma_start(kbd[HD * j:HD * (j + 1), :, N * j:N * (j + 1)].bitcast(F32),
                                 k_dram[0, HD * j:HD * (j + 1), :, batch, :]).then_inc(kbd_in, DMA)

            def stack_low(a, b, done):
                for j in range(J):
                    sp.dma_start(qs[HD:2 * HD, j, a:b].bitcast(F32),
                                 ql[HD * j:HD * (j + 1), a:b].bitcast(F32)).then_inc(done, DMA)

            def stack_high():
                for row in (0, 2 * HD):
                    for j in range(J):
                        sp.dma_start(qs[row:row + HD, j].bitcast(F32),
                                     qh[HD * j:HD * (j + 1)].bitcast(F32)).then_inc(q_in, DMA)

            def stack_max():
                for part in range(2):
                    sp.dma_start(qs[3 * HD + part:3 * HD + part + 1].bitcast(F32)
                                 .rearrange("p j g t -> p (j g) t"),
                                 mrow[HEADS * part:HEADS * (part + 1), :]).then_inc(m_in, DMA)

            sp.dma_start(c_raw, ctx.rearrange("b n l -> n b l")).then_inc(ctx_in, DMA)
            sp.dma_start(xn[:], tokens(xf, 0)).then_inc(x_in, DMA)
            for dst, src in ((tg, tnorm_g), (tb, tnorm_b), (bks, bk)):
                sp.dma_start(dst, src).then_inc(kv_vec_in, DMA)
            for dst, src in ((ng, norm_g), (nb, norm_b), (bqs[:], bq), (b1s[:], b1)):
                sp.dma_start(dst, src).then_inc(vec_in, DMA)
            sp.dma_start(wq_raw, Wq.rearrange("(c p) n -> p c n", p=P)).then_inc(wq_in, DMA)
            sp.dma_start(wk_raw, Wk.rearrange("(c p) n -> p c n", p=P)).then_inc(wk_in, DMA)
            sp.dma_start(wv_raw, Wv.rearrange("(c p) n -> p c n", p=P)).then_inc(wv_in, DMA)
            sp.dma_start(bv_all, bv.rearrange("(a d) -> a d", a=1).to_broadcast([N, D])).then_inc(row_in, DMA)
            sp.dma_start(u1_raw, U1.rearrange("(c p) n -> p c n", p=P)).then_inc(ffn_in, DMA)
            sp.dma_start(v2_raw, V2).then_inc(ffn_in, DMA)
            sp.dma_start(u2_raw, U2.rearrange("(c p) n -> p c n", p=P)).then_inc(ffn_in, DMA)
            sp.dma_start(v1_raw, V1).then_inc(v1_in, DMA)
            sp.wait_ge(pair_full, T1_FIRST + DC)
            sp.dma_start(xn[:], tokens(xf, 1)).then_inc(x_in, DMA)
            sp.wait_ge(setup_dve, KEYS_DONE)
            sp.wait_ge(cleared, 2)
            for j in range(J):
                sp.dma_start(kbd[HD * j:HD * (j + 1), :, N * j:N * (j + 1)].bitcast(F32),
                             k_hl[HD * j:HD * (j + 1), :, 0, 0:N].bitcast(F32)).then_inc(kbd_in, DMA)
            for row, part in ((0, 0), (HD, 0), (2 * HD, 1)):
                for j in range(J):
                    sp.dma_start(ks[row:row + HD, j].bitcast(F32),
                                 k_hl[HD * j:HD * (j + 1), :, part, 0:N].bitcast(F32)).then_inc(ks_in, DMA)
            for part in range(2):
                sp.dma_start(k_dram[part].rearrange("p g b n -> p g (b n)"),
                             k_hl[:, :, part, :].bitcast(F32)).then_inc(k_saved, DMA)
            sp.wait_ge(setup_dve, KEYS_DONE + 1)
            sp.dma_start(v_dram[1], v_other.rearrange("n h i w -> n (h i w)")).then_inc(v_other_saved, DMA)
            sp.wait_ge(pair_lo, Q_FIRST + G)
            stack_low(0, G, ql_in)
            stack_high()
            sp.wait_ge(dv_free, PROLOGUE_DV)
            stack_max()
            sp.wait_ge(setup_dve, KEYS_DONE + B)
            sp.dma_start(v_dram[0], vs[:].rearrange("n h i w -> n (h i w)")).then_inc(v_saved, DMA)
            sp.dma_start(b2_all[:], b2.rearrange("(a d) -> a d", a=1).to_broadcast([P, D])).then_inc(row_in, DMA)

            def body(t):
                k = t.k
                if t is not first:
                    sp.wait_ge(out_done, DMA * k)
                else:
                    sp.wait_ge(k_saved, DMA * 2)
                    sp.wait_ge(v_saved, DMA)
                    sp.wait_ge(v_other_saved, DMA)
                    sp.wait_ge(w_lo, FFN_WEIGHTS)
                sp.dma_start(x1[:], tokens(xf, k)).then_inc(x1_in, DMA)
                if t.next_batch != t.batch:
                    sp.wait_ge(dv_full, t.pv)
                    load_diagonal(t.next_batch)
                    sp.wait_ge(sc_full, t.sb + HEADS)
                    load_keys(t.next_batch)
                    sp.wait_ge(dv_full, t.pv + 2 * TT)
                    sp.dma_start(vs[:].rearrange("n h i w -> n (h i w)"), v_dram[t.next_batch]).then_inc(vs_in, DMA)
                if t.has_next:
                    sp.wait_ge(pair_lo, t.q[1] + 1)
                    stack_low(0, G // 2, ql_in)
                if t.has_x:
                    sp.wait_ge(pair_full, t.t2 + DC)
                    sp.dma_start(xn[:], tokens(xf, k + 2)).then_inc(x_in, DMA)
                if t.has_next:
                    sp.wait_ge(pair_lo, t.q[G - 1] + 1)
                    stack_low(G // 2, G, ql_last_in)
                    stack_high()
                    sp.wait_ge(dv_free, t.mt + TT)
                    stack_max()
                if t.has_next:
                    sp.wait_ge(dv_free, t.v2 + TT)
                    sp.dma_start(tokens(of, k), x1[:]).then_inc(out_done, DMA)
                else:
                    for tt in range(TT):
                        sp.wait_ge(dv_free, t.v2 + tt + 1)
                        sp.dma_start(of[k * TB + P * tt:k * TB + P * (tt + 1), :], x1[:, tt, :]).then_inc(out_done, DMA)

            run(sp, body)
            sp.wait_ge(out_done, DMA * (BLOCKS - 1 + TT))

        @block.tensor
        def _(pe):
            def three(o, w, m, first_pass, last_pass, low_done=None, low_count=0):
                pe.matmul(o, w(0), m(0), start=first_pass, stop=False)
                pe.matmul(o, w(1), m(0), start=False, stop=False)
                if low_done is not None:
                    pe.wait_ge(low_done, low_count)
                return pe.matmul(o, w(0), m(1), start=False, stop=last_pass)

            def pair_bank(use, u):
                at_least(pe, pair_lo, use - 1)
                return pair[u % 2]

            def dv_bank(use, u):
                at_least(pe, dv_free, use - 3)
                return dv[u % 4]

            def turn_x(bank, c, tiles=range(TT)):
                for tt in tiles:
                    mm = pe.transpose(bank[:, P * tt:P * (tt + 1)], xn[:, tt, P * c:P * (c + 1)], ident[:])
                return mm

            def project_q(use, g, c, bank, x_use):
                if g == 0:
                    pe.wait_ge(pair_hi, x_use + c + 1)
                mm = three(bank[:], lambda i: wq[:, i, c, P * g:P * (g + 1)],
                           lambda i: xt[:, i, c, :], c == 0, c == DC - 1,
                           pair_lo if g == 0 else None, x_use + c + 1)
                if c == DC - 1:
                    mm.then_inc(pair_full, 1)

            def max_pass(use, s):
                g, tt = divmod(s, TT)
                bank = dv_bank(use + s, s)
                pe.matmul(bank[:, 0:J * N], qh[:, g, P * tt:P * (tt + 1)], kbd[:, g, :],
                          start=True, stop=True).then_inc(dv_full, 1)

            def turn_max(use, blk):
                pe.wait_ge(m_lo, blk + 1)
                at_least(pe, dv_free, use - 3)
                for tt in range(TT):
                    mm = pe.transpose(dv[0][0:2 * HEADS, P * tt:P * (tt + 1)], msp[:, tt, :], ident[:])
                mm.then_inc(dv_full, TT)

            def scores(t, h):
                g, j = divmod(h, J)
                if t.has_next and h < 3:
                    chunk = (None, 0, 1)[h] if t is first else (1, 0, 2)[h]
                    if chunk is not None:
                        pe.wait_ge(pair_lo, t.x_use + chunk + 1)
                at_least(pe, sc_done, t.sb + h - 2)
                bank = score_banks[h % 3]
                if h == 0:
                    pe.wait_ge(q_in, DMA * Q_DMAS * (t.k + 1))
                    pe.wait_ge(ql_in, DMA * QL_DMAS * (t.k + 1))
                    at_least(pe, ql_last_in, DMA * QL_DMAS * t.k)
                    pe.wait_ge(m_in, DMA * 2 * (t.k + 1))
                    pe.wait_ge(ks_in, DMA * K_DMAS * (t.batch + 1))
                pe.matmul(bank[0:N, :], ks[:, j, g, :], qs[0:KS, j, g, :],
                          start=True, stop=True).then_inc(sc_full, 1)

            def weights_values(t, half, tt, h):
                o = dv[tt][:, VW * (h - HALF * half):VW * (h - HALF * half + 1)]
                w = [pw[0:N, i, TB * h + P * tt:TB * h + P * (tt + 1)] for i in range(2)]
                terms = [(0, 0), (0, 1), (0, 2), (1, 0), (1, 1)]
                for n, (i, v) in enumerate(terms):
                    mm = pe.matmul(o, w[i], vs[:, h, v, :], start=(n == 0), stop=(n == len(terms) - 1))
                return mm

            def weights_ready(t, h):
                pe.wait_ge(pl_odd if h % 2 else pl_even, HALF * t.k + h // 2 + 1)

            def output_rows(t, tt):
                if t.has_next and tt == TT - 1:
                    pe.wait_ge(dv_free, t.mt + TT)
                bank = dv[(tt + 1) % TT]
                rows = slice(P * tt, P * (tt + 1))
                pe.matmul(bank[:], mid[:, 0, rows], v2[:, 0, :], start=True, stop=False)
                pe.matmul(bank[:], mid[:, 0, rows], v2[:, 1, :], start=False, stop=False)
                if tt == 0:
                    pe.wait_ge(pair_lo, t.pu2 + 1)
                pe.matmul(bank[:], mid[:, 1, rows], v2[:, 0, :], start=False, stop=True).then_inc(dv_full, 1)

            pe.wait_ge(consts, 1)
            pe.wait_ge(setup_step, 1)
            for c in range(LC):
                for b in range(B):
                    mm = pe.transpose(dv[c][:, N * b:N * (b + 1)], c_nrm[:, b, P * c:P * (c + 1)], ident[0:N, 0:N])
                mm.then_inc(setup_pe, 1)
            pe.wait_ge(wq_in, DMA)
            pe.wait_ge(vec_in, DMA * 4)
            for c in range(DC):
                mm = pe.matmul(dv[3][0:1, :], nb[:, c:c + 1], wq_raw[:, c, :], start=(c == 0), stop=(c == DC - 1))
            mm.then_inc(setup_pe, 1)

            def keys(g):
                for c in range(LC):
                    mm = pe.matmul(key_banks[g][:, 0:B * N], wk_raw[:, c, P * g:P * (g + 1)], c_t[:, c, :],
                                   start=(c == 0), stop=(c == LC - 1))
                mm.then_inc(setup_pe, 1)

            def values(b, bank):
                for c in range(LC):
                    mm = pe.matmul(bank[0:N, :], c_t[:, c, N * b:N * (b + 1)], wv_raw[:, c, :],
                                   start=(c == 0), stop=(c == LC - 1))
                mm.then_inc(setup_pe, 1)

            pe.wait_ge(norm1, TT)
            for c in range(DC):
                turn_x(pair_bank(T1_FIRST + c, c), c).then_inc(pair_full, 1)
                if c == 0:
                    pe.wait_ge(row_out, 1)
                    for g in range(G):
                        mm = pe.transpose(sc[1][:, g:g + 1], bias_row[:, P * g:P * (g + 1)], ident[0:1, 0:1])
                    mm.then_inc(setup_pe, 1)
                if c == 1:
                    pe.wait_ge(wk_in, DMA)
                    pe.wait_ge(setup_dve, LC)
                    keys(0)
                    keys(1)
            keys(2)
            keys(3)
            pe.wait_ge(wq_lo, 1)
            for g in range(G):
                if g == 2:
                    pe.wait_ge(wv_in, DMA)
                    pe.wait_ge(setup_dve, BIAS_DONE)
                    values(1, sc[1])
                for c in range(DC):
                    if c == 0:
                        pair_bank(Q_FIRST + g, g)
                    project_q(Q_FIRST + g, g, c, pair[g % 2], T1_FIRST)
            pe.wait_ge(pair_hi, Q_FIRST + G)
            pe.wait_ge(kbd_in, DMA * KBD_DMAS)
            pe.wait_ge(setup_dve, KEYS_DONE + 1)
            for s in range(TT * G):
                max_pass(0, s)
                if s == TT * G // 2:
                    pe.wait_ge(norm1, TT * 2)
                    pe.wait_ge(pair_lo, Q_FIRST + G)
                if s >= TT * G // 2 and s % 2 == 0 and s < TT * G - 2:
                    c = (s - TT * G // 2) // 2
                    turn_x(t1_second_banks[c], c).then_inc(pair_full, 1)
            turn_max(TT * G, 0)
            values(0, dv[1])
            turn_x(t1_second_banks[3], 3).then_inc(pair_full, 1)
            pe.wait_ge(w_lo, 2)
            pe.wait_ge(k_saved, DMA * 2)
            pe.wait_ge(v_other_saved, DMA)

            def body(t):
                k = t.k
                for h in range(HEADS):
                    if t is first and h == HALF - 2:
                        pe.wait_ge(setup_dve, KEYS_DONE + B)
                    if t is first and h == HALF:
                        pe.wait_ge(w_lo, 3)
                    scores(t, h)
                    if h < HALF:
                        if t.has_next and h in (2, 4, 6, 7):
                            if h == 2:
                                pe.wait_ge(pair_lo, t.x_use + DC)
                            project_q(t.q[0], 0, (2, 4, 6, 7).index(h), q_banks[0], t.x_use)
                    else:
                        if h == HALF:
                            pe.wait_ge(dv_free, t.pv)
                            at_least(pe, vs_in, DMA * t.batch)
                        weights_ready(t, h - HALF)
                        for tt in range(TT):
                            mm = weights_values(t, 0, tt, h - HALF)
                            if h == HEADS - 1:
                                mm.then_inc(dv_full, 1)
                if t.has_next:
                    pe.wait_ge(sc_done, t.sb + HEADS - 2)
                    for c in range(DC):
                        project_q(t.q[1], 1, c, q_banks[1], t.x_use)
                for tt in range(TT):
                    for h in range(HALF, HEADS):
                        if tt == 0:
                            weights_ready(t, h)
                        if h == HALF:
                            pe.wait_ge(dv_free, t.pv + tt + 1)
                        mm = weights_values(t, 1, tt, h)
                    mm.then_inc(dv_full, 1)
                if t.has_next:
                    pe.wait_ge(pair_lo, t.q[0] + 1)
                    for c in range(DC):
                        project_q(t.q[2], 2, c, q_banks[2], t.x_use)
                    pe.wait_ge(dv_free, t.pv + 2 * TT)
                    for c in range(3):
                        project_q(t.q[3], 3, c, q_banks[3], t.x_use)
                pe.wait_ge(sc_done, t.sb + HEADS)
                pe.wait_ge(dv_free, t.pv + TT + 2)
                pe.wait_ge(norm2_act, t.norm2)
                for c in range(DC):
                    turn_x(t2_banks[c], c, range(0, TT // 2))
                pe.wait_ge(norm2_dve, t.norm2)
                for c in range(DC):
                    turn_x(t2_banks[c], c, range(TT // 2, TT)).then_inc(pair_full, 1)
                if t.has_next:
                    project_q(t.q[3], 3, 3, q_banks[3], t.x_use)
                if t is first:
                    pe.wait_ge(w_lo, FFN_WEIGHTS)
                if t.has_next:
                    pe.wait_ge(pair_lo, t.q[1] + 1)
                for c in range(DC):
                    pe.wait_ge(pair_hi, t.t2 + c + 1)
                    mm = three(pair[0][:], lambda i: u1[:, i, c, :], lambda i: x1t[:, i, c, :], c == 0, c == DC - 1,
                               pair_lo, t.t2 + c + 1)
                mm.then_inc(pair_full, 1)
                if t.has_next:
                    pe.wait_ge(kbd_in, DMA * KBD_DMAS * (t.next_batch + 1))
                    for s in range(MAX_AHEAD):
                        if s == 2:
                            pe.wait_ge(pair_lo, t.q[G - 1] + 1)
                        max_pass(t.sa, s)
                pe.wait_ge(pair_hi, t.pu1 + 1)
                for s in range(FC + LAG):
                    if s < FC:
                        if s >= 3:
                            pe.wait_ge(sc_done, t.v1 + s - 2)
                        three(hidden_banks[s % 3][:], lambda i: v1[:, i, P * s:P * (s + 1)], lambda i: mid[:, i, :],
                              True, True, pair_lo if s == 0 else None, t.pu1 + 1).then_inc(sc_full, 1)
                        if t.has_next and s + MAX_AHEAD < TT * G:
                            if s + MAX_AHEAD == (G - 1) * TT:
                                pe.wait_ge(pair_hi, t.q[G - 1] + 1)
                            max_pass(t.sa, s + MAX_AHEAD)
                    if t.has_next and s == FC:
                        turn_max(t.mt, k + 1)
                    if s >= LAG:
                        f = s - LAG
                        if f == 0:
                            acc = pair[1]
                        if f % 2:
                            pe.wait_ge(h_hi, FC // 2 * k + f // 2 + 1)
                        else:
                            pe.wait_ge(sc_done, t.v1 + f + 1)
                        mm = three(acc[:], lambda i: u2[:, i, f, :], lambda i: x1t[:, i, f % 4, :],
                                   f == 0, f == FC - 1,
                                   h_odd if f % 2 else h_even, FC // 2 * k + f // 2 + 1)
                        mm.then_inc(u2_done if f < FC - 1 else pair_full, 1)
                    if t.has_x and s == FC + LAG - 2:
                        pe.wait_ge(norm1, TT * (k + 3))
                        pe.wait_ge(sc_done, t.v1 + FC - 1)
                        turn_x(t1_banks[0], 0).then_inc(pair_full, 1)
                if t.has_x:
                    for c in range(1, 3):
                        pe.wait_ge(sc_done, t.v1 + FC)
                        turn_x(t1_banks[c], c).then_inc(pair_full, 1)
                pe.wait_ge(pair_hi, t.pu2 + 1)
                for tt in range(TT):
                    output_rows(t, tt)
                    if t.has_x and tt == 0:
                        turn_x(t1_banks[DC - 1], DC - 1).then_inc(pair_full, 1)

            run(pe, body)

        @block.scalar
        def _(act):
            def high(use, bank, o, bias=None):
                act.wait_ge(pair_full, use + 1)
                if bias is None:
                    act.activation(o, bank[:], ACT.Copy).then_inc(pair_hi, 1)
                else:
                    act.activation(o, bank[:], ACT.Identity, bias=bias).then_inc(pair_hi, 1)

            def load_table(func, n):
                at_least(act, tables_in, n)
                act.activation(tables[:], mhalf[:, 0:1], func).then_inc(tables_in, 1)

            def normalise(tt):
                act.activation(xn[:, tt, :], xn[:, tt, :], ACT.Identity, bias=ln1[:, 5, tt:tt + 1],
                               scale=ln1[:, 4, tt:tt + 1]).then_inc(norm1, 1)

            act.wait_ge(wq_in, DMA)
            act.wait_ge(vec_in, DMA * 4)
            for c in range(DC):
                act.activation(wq[:, 0, c, :], wq_raw[:, c, :], ACT.Identity, scale=ng[:, c:c + 1]).then_inc(wq_hi, 1)
            act.wait_ge(ln1_step, LN1_STEPS)
            for tt in range(TT // 2, TT):
                normalise(tt)
            for c in range(DC):
                high(T1_FIRST + c, pair[c % 2], xt[:, 0, c, :])
            act.wait_ge(setup_dve, BIAS_DONE)
            for g in range(G):
                high(Q_FIRST + g, pair[g % 2], qh[:, g, :], q_bias[:, g:g + 1])
                if g == 0:
                    act.wait_ge(ffn_in, DMA * 3)
                    act.copy(u1[:, 0], u1_raw).then_inc(w_hi, 1)
                    act.copy(v2[:, 0], v2_raw).then_inc(w_hi, 1)
                    act.copy(u2[:, 0], u2_raw).then_inc(w_hi, 1)
                if g == 1:
                    act.wait_ge(v1_in, DMA)
                    act.copy(v1[:, 0], v1_raw).then_inc(w_hi, 1)
            act.wait_ge(ln1_step, LN1_STEPS * 2)
            for tt in range(TT // 2, TT):
                normalise(tt)
            for c in range(DC):
                high(T1_SECOND + c, t1_second_banks[c], xt[:, 0, c, :])
            load_table(ACT.Exp, 0)

            def body(t):
                k = t.k
                for h in range(HEADS):
                    act.wait_ge(sc_full, t.sb + h + 1)
                    at_least(act, pl_odd if h % 2 else pl_even, HALF * k + (h - 4) // 2 + 1)
                    ins = act.activation(pt[:, h % 4, :], score_banks[h % 3][0:N, :], ACT.Exp)
                    if h % 4 == 0:
                        ins = act.activation(pw[0:N, 0, TB * h:TB * (h + 1)], score_banks[h % 3][0:N, :], ACT.Exp)
                    ins.then_inc(sc_done, 1)
                    if t.has_next and h == 7:
                        act.wait_ge(q_in, DMA * Q_DMAS * (k + 1))
                        high(t.q[0], q_banks[0], qh[:, 0, :], q_bias[:, 0:1])
                load_table(ACT.Gelu_apprx_tanh, 2 * k + 1)
                if t.has_next:
                    high(t.q[1], q_banks[1], qh[:, 1, :], q_bias[:, 1:2])
                act.wait_ge(ln2_step, LN2_STEPS * k + 4)
                for tt in range(2):
                    act.activation(xn[:, tt, :], x1[:, tt, :], ACT.Identity, bias=ln2[:, 3, tt:tt + 1],
                                   scale=ln2[:, 1, tt:tt + 1]).then_inc(norm2_act, 1)
                if t.has_next:
                    high(t.q[2], q_banks[2], qh[:, 2, :], q_bias[:, 2:3])
                for c in range(DC):
                    high(t.t2 + c, t2_banks[c], x1t[:, 0, c, :])
                if t.has_next:
                    high(t.q[3], q_banks[3], qh[:, 3, :], q_bias[:, 3:4])
                high(t.pu1, pair[0], mid[:, 0, :])
                if t.has_next:
                    act.wait_ge(ql_in, DMA * QL_DMAS * (k + 2))
                for f in range(FC):
                    act.wait_ge(sc_full, t.v1 + f + 1)
                    if t.has_next and f == G // 2:
                        act.wait_ge(ql_last_in, DMA * QL_DMAS * (k + 1))
                    if f >= 4:
                        act.wait_ge(u2_done, (FC - 1) * k + f - 3)
                    ins = act.activation(ql[:, f % 4, :], hidden_banks[f % 3][:], ACT.Gelu_apprx_tanh,
                                         bias=b1s[:, f:f + 1])
                    if f % 2 == 0:
                        ins = act.activation(x1t[:, 0, f % 4, :], hidden_banks[f % 3][:], ACT.Gelu_apprx_tanh,
                                             bias=b1s[:, f:f + 1])
                    ins.then_inc(sc_done, 1)
                    if t.has_x and f in (FC - 4, FC - 3):
                        if f == FC - 4:
                            act.wait_ge(ln1_step, LN1_STEPS * (k + 3))
                        normalise(f - (FC - 4))
                if t.has_x:
                    high(t.t1[0], t1_banks[0], xt[:, 0, 0, :])
                high(t.pu2, pair[1], mid[:, 0, :])
                if t.has_next:
                    load_table(ACT.Exp, 2 * k + 2)
                if t.has_x:
                    for c in range(1, DC):
                        high(t.t1[c], t1_banks[c], xt[:, 0, c, :])

            run(act, body)

        @block.vector
        def _(dve):
            def low(use, bank, o, hi, bias=None):
                dve.wait_ge(pair_hi, use + 1)
                if bias is None:
                    dve.tensor_tensor(o, bank[:], hi.bitcast(F32), ALU.subtract).then_inc(pair_lo, 1)
                else:
                    dve.scalar_tensor_tensor(out=o, in0=bank[:], scalar=bias, in1=hi.bitcast(F32),
                                             op0=ALU.add, op1=ALU.subtract).then_inc(pair_lo, 1)

            def stats(src, st, mv, part, done, n):
                for tt in range(TT):
                    ins = dve.bn_stats(st[:, tt, :], src[:, tt, :])
                ins.then_inc(part, 1)
                dve.wait_ge(part, n + 1)
                dve.nop().then_inc(dve_waited, 1)
                for tt in range(TT):
                    ins = dve.bn_aggr(mv[:, tt, :], st[:, tt, :])
                ins.then_inc(done, 1)

            def reduce_max(use, s):
                g, tt = divmod(s, TT)
                dve.wait_ge(dv_full, use + s + 1)
                o = mneg[:, tt, :].rearrange("p (j g) -> p j g", j=J)[:, :, g]
                dve.tensor_reduce(o, dv[s % 4][:, 0:J * N].rearrange("p (j n) -> p j n", j=J), AX.X, ALU.max,
                                  negate=True).then_inc(dv_free, 1)

            def split_max(blk, use):
                dve.wait_ge(dv_free, use)
                hi, lo = msp[:, :, 0:HEADS], msp[:, :, HEADS:2 * HEADS]
                dve.tensor_copy(hi.bitcast(F32R), mneg).then_inc(m_hi, 1)
                dve.wait_ge(m_hi, blk + 1)
                dve.tensor_tensor(lo.bitcast(F32R), mneg, hi, ALU.subtract).then_inc(m_lo, 1)

            def save_max(blk, use):
                at_least(dve, m_in, DMA * 2 * blk)
                dve.wait_ge(dv_full, use + TT)
                dve.tensor_copy(mrow, dv[0][0:2 * HEADS, :]).then_inc(dv_free, TT)

            dve.wait_ge(ctx_in, DMA)
            for b in range(B):
                ins = dve.bn_stats(st2[0:N, b, 0, :], c_raw[:, b, :])
            ins.then_inc(ctx_stats, 1)
            dve.wait_ge(ctx_stats, 1)
            for b in range(B):
                ins = dve.bn_aggr(mv2[0:N, b, :], st2[0:N, b, 0, :])
            ins.then_inc(ctx_stats, 1)
            dve.wait_ge(ctx_coef, 2)
            for b in range(B):
                ins = dve.tensor_scalar(c_nrm[:, b, :], c_raw[:, b, :], mv2[0:N, b, 0:1], ln2[0:N, 1, b:b + 1],
                                        ALU.subtract, ALU.mult)
            ins.then_inc(setup_step, 1)
            dve.wait_ge(x_in, DMA)
            stats(xn, st1, mv1, st1_part, st1_done, 0)
            dve.wait_ge(kv_vec_in, DMA * 3)
            for c in range(LC):
                dve.wait_ge(setup_pe, c + 1)
                dve.tensor_scalar(c_t[:, c, :], dv[c][:, 0:B * N], tg[:, c:c + 1], tb[:, c:c + 1],
                                  ALU.mult, ALU.add).then_inc(setup_dve, 1)
            for c in range(DC):
                dve.wait_ge(wq_hi, c + 1)
                ins = dve.scalar_tensor_tensor(out=wq[:, 1, c, :], in0=wq_raw[:, c, :], scalar=ng[:, c:c + 1],
                                               in1=wq[:, 0, c, :].bitcast(F32), op0=ALU.mult, op1=ALU.subtract)
            ins.then_inc(wq_lo, 1)
            dve.wait_ge(setup_pe, LC + 1)
            dve.tensor_copy(bias_row, dv[3][0:1, :]).then_inc(row_out, 1)
            low(T1_FIRST, pair[0], xt[:, 1, 0, :], xt[:, 0, 0, :])
            dve.wait_ge(setup_pe, LC + 2)
            dve.tensor_tensor(q_bias[:], sc[1][:, 0:DC], bqs[:], ALU.add).then_inc(setup_dve, 1)
            for c in range(1, DC):
                low(T1_FIRST + c, pair[c % 2], xt[:, 1, c, :], xt[:, 0, c, :])
            for g in range(G):
                dve.wait_ge(setup_pe, LC + 2 + G)
                dve.wait_ge(setup_dve, BIAS_DONE + g)
                dve.tensor_scalar(kf, key_banks[g][:, 0:B * N], bks[:, g:g + 1], SCALE,
                                  ALU.add, ALU.mult).then_inc(m_red, 1)
                dve.wait_ge(m_red, 2 * g + 1)
                dve.tensor_copy(k_hl[:, g, 0, :], kf).then_inc(m_red, 1)
                dve.wait_ge(m_red, 2 * g + 2)
                dve.tensor_tensor(k_hl[:, g, 1, :], kf, k_hl[:, g, 0, :].bitcast(F32), ALU.subtract).then_inc(setup_dve, 1)
            def values(b):
                n = B - 1 - b
                step = 2 * G + 5 * n
                dve.wait_ge(setup_pe, LC + 2 + G + n + 1)
                dve.tensor_tensor(vf[b], (dv[1] if b == 0 else sc[1])[0:N, :], bv_all, ALU.add).then_inc(m_red, 1)
                rest = vf[b].rearrange("n (h d) -> n h d", h=HEADS)
                for i in range(3):
                    part = (vs if b == 0 else v_other)[:, :, i, 0:HD]
                    dve.wait_ge(m_red, step + 2 * i + 1)
                    ins = dve.tensor_copy(part, rest)
                    if i < 2:
                        ins.then_inc(m_red, 1)
                        dve.wait_ge(m_red, step + 2 * i + 2)
                        dve.tensor_tensor(rest, rest, part, ALU.subtract).then_inc(m_red, 1)
                    else:
                        ins.then_inc(setup_dve, 1)

            for g in range(G):
                low(Q_FIRST + g, pair[g % 2], ql[:, g, :].bitcast(F32R), qh[:, g, :], q_bias[:, g:g + 1])
                if g == 0:
                    dve.wait_ge(x_in, DMA * 2)
                    stats(xn, st1, mv1, st1_part, st1_done, 1)
                if g == 1:
                    dve.wait_ge(row_in, DMA)
                    dve.wait_ge(cleared, 3)
                    values(1)
            dve.wait_ge(w_lo, 2)
            for s in range(TT * G):
                reduce_max(0, s)
            split_max(0, TT * G)
            save_max(0, TT * G)
            for c in range(3):
                low(T1_SECOND + c, t1_second_banks[c], xt[:, 1, c, :], xt[:, 0, c, :])
            values(0)
            low(T1_SECOND + 3, t1_second_banks[3], xt[:, 1, 3, :], xt[:, 0, 3, :])

            def output_rows(blk, use, tt):
                if tt == 0:
                    dve.wait_ge(x1_b2, TT * (blk + 1))
                dve.wait_ge(dv_full, use + tt + 1)
                dve.tensor_tensor(x1[:, tt, :], dv[(tt + 1) % TT][:], x1[:, tt, :], ALU.add).then_inc(dv_free, 1)

            def divide(t, half, tt):
                bank = dv[tt][:, 0:HALF * VW].rearrange("p (h w) -> p h w", w=VW)
                u = TT * half + tt
                dve.wait_ge(dv_full, t.pv + u + 1)
                dve.reciprocal(rinv[:, tt % 2, :], bank[:, :, HD]).then_inc(rinv_done, 1)
                dve.wait_ge(rinv_done, 2 * TT * t.k + u + 1)
                dve.tensor_tensor(y_half[tt].rearrange("p (h d) -> p h d", d=HD), bank[:, :, 0:HD],
                                  rinv[:, tt % 2, :].unsqueeze(2).to_broadcast([P, HALF, HD]),
                                  ALU.mult).then_inc(dv_free, 1)

            def body(t):
                k = t.k
                for h in range(HEADS):
                    if h % 4:
                        dve.wait_ge(sc_done, t.sb + h + 1)
                        hi, lo = (pw[0:N, i, TB * h:TB * (h + 1)] for i in range(2))
                        dve.tensor_copy(hi, pt[:, h % 4, :]).then_inc(ph_done, 1)
                        if h % 2:
                            dve.wait_ge(ph_done, PH * k + 3 * (h // 4) + h % 4)
                            dve.tensor_tensor(lo, pt[:, h % 4, :], hi, ALU.subtract).then_inc(pl_odd, 1)
                    if t.has_next and h == 9:
                        low(t.q[0], q_banks[0], ql[:, 0, :].bitcast(F32R), qh[:, 0, :], q_bias[:, 0:1])
                for tt in range(TT):
                    divide(t, 0, tt)
                for tt in range(TT + 1):
                    if tt < TT:
                        dve.wait_ge(x1_half, TT * k + tt + 1)
                        dve.bn_stats(st2[:, tt, 0, :], x1[:, tt, 0:D // 2])
                        divide(t, 1, tt)
                    else:
                        dve.wait_ge(dv_free, t.pv + 2 * TT)
                        part = x1[:, TT - 1, D // 2:D]
                        dve.tensor_tensor(part, part, y_half[TT - 1], ALU.add).then_inc(x1_sum, 1)
                    if tt:
                        done = tt - 1
                        dve.wait_ge(x1_sum, TT * k + done + 1)
                        ins = dve.bn_stats(st2[:, done, 1, :], x1[:, done, D // 2:D])
                        if done % 2:
                            ins.then_inc(st2_part, 1)
                            dve.wait_ge(st2_part, 2 * k + done // 2 + 1)
                            dve.nop().then_inc(dve_waited, 1)
                            for i in (done - 1, done):
                                ins = dve.bn_aggr(mv2[:, i, :], st2[:, i, :, :])
                            ins.then_inc(st2_done, 1)
                if t.has_next:
                    low(t.q[1], q_banks[1], ql[:, 1, :].bitcast(F32R), qh[:, 1, :], q_bias[:, 1:2])
                dve.wait_ge(ln2_step, LN2_STEPS * (k + 1))
                for tt in range(TT // 2, TT):
                    dve.tensor_scalar(xn[:, tt, :], x1[:, tt, :], mv2[:, tt, 0:1], ln2[:, 1, tt:tt + 1],
                                      ALU.subtract, ALU.mult).then_inc(norm2_dve, 1)
                if t.has_next:
                    low(t.q[2], q_banks[2], ql[:, 2, :].bitcast(F32R), qh[:, 2, :], q_bias[:, 2:3])
                for c in range(DC):
                    low(t.t2 + c, t2_banks[c], x1t[:, 1, c, :], x1t[:, 0, c, :])
                if t.has_next:
                    low(t.q[3], q_banks[3], ql[:, 3, :].bitcast(F32R), qh[:, 3, :], q_bias[:, 3:4])
                low(t.pu1, pair[0], mid[:, 1, :], mid[:, 0, :])
                if t.has_next:
                    for s in range(MAX_AHEAD):
                        reduce_max(t.sa, s)
                for f in range(FC):
                    if f % 2:
                        dve.wait_ge(sc_done, t.v1 + f + 1)
                        if f >= 4:
                            dve.wait_ge(u2_done, (FC - 1) * k + f - 3)
                        dve.tensor_copy(x1t[:, 0, f % 4, :], ql[:, f % 4, :]).then_inc(h_hi, 1)
                    if t.has_next and f + MAX_AHEAD < TT * G:
                        reduce_max(t.sa, f + MAX_AHEAD)
                    if f % 2:
                        dve.wait_ge(h_hi, FC // 2 * k + f // 2 + 1)
                        dve.tensor_tensor(x1t[:, 1, f % 4, :], ql[:, f % 4, :], x1t[:, 0, f % 4, :].bitcast(F32),
                                          ALU.subtract).then_inc(h_odd, 1)
                    if t.has_x and f in (FC - 3, FC - 2):
                        if f == FC - 3:
                            dve.wait_ge(ln1_step, LN1_STEPS * (k + 3))
                        tt = f - (FC - 3) + TT // 2
                        dve.tensor_scalar(xn[:, tt, :], xn[:, tt, :], ln1[:, 4, tt:tt + 1], ln1[:, 5, tt:tt + 1],
                                          ALU.mult, ALU.add).then_inc(norm1, 1)
                    if t.has_next and f == TT * G - MAX_AHEAD:
                        split_max(k + 1, t.sa + TT * G)
                    if t.has_x:
                        if f == 1:
                            dve.wait_ge(x_in, DMA * (k + 3))
                        if 1 <= f < 1 + TT:
                            ins = dve.bn_stats(st1[:, f - 1, :], xn[:, f - 1, :])
                        if f == TT:
                            ins.then_inc(st1_part, 1)
                        if f == 1 + TT:
                            dve.wait_ge(st1_part, k + 3)
                            dve.nop().then_inc(dve_waited, 1)
                            for tt in range(TT):
                                ins = dve.bn_aggr(mv1[:, tt, :], st1[:, tt, :])
                            ins.then_inc(st1_done, 1)
                if t.has_next:
                    save_max(k + 1, t.mt)
                if t.has_x:
                    low(t.t1[0], t1_banks[0], xt[:, 1, 0, :], xt[:, 0, 0, :])
                low(t.pu2, pair[1], mid[:, 1, :], mid[:, 0, :])
                for tt in range(TT):
                    chunks = {0: (1, 2), 1: (3,)}.get(tt, ())
                    if t.has_x:
                        for c in chunks:
                            low(t.t1[c], t1_banks[c], xt[:, 1, c, :], xt[:, 0, c, :])
                    output_rows(k, t.v2, tt)

            run(dve, body)

        @block.gpsimd
        def _(pool):
            def coefficients1(n, part=None):
                mean, var = mv1[:, :, 0], mv1[:, :, 1]
                s = LN1_STEPS * n
                if part in (None, 0):
                    coefficients1_first(var, s)
                if part in (None, 1):
                    coefficients1_second(var, s)
                if part in (None, 2):
                    coefficients1_third(mean, s)

            def coefficients1_first(var, s):
                pool.nop().then_inc(pool_waited, 1)
                pool.tensor_scalar(ln1[:, 0, :], var, EPS, 1.0, ALU.add, ALU.mult).then_inc(ln1_step, 1)
                pool.wait_ge(ln1_step, s + 1)
                pool.tensor_tensor(ln1[:, 1, :], ln1[:, 0, :], mhalf[:, 0:TT], ALU.pow).then_inc(ln1_step, 1)

            def coefficients1_second(var, s):
                pool.wait_ge(ln1_step, s + 2)
                pool.tensor_tensor(ln1[:, 2, :], var, ln1[:, 1, :], ALU.mult).then_inc(ln1_step, 1)
                pool.wait_ge(ln1_step, s + 3)
                pool.tensor_tensor(ln1[:, 3, :], ln1[:, 2, :], ln1[:, 1, :], ALU.mult).then_inc(ln1_step, 1)
                pool.wait_ge(ln1_step, s + 4)
                pool.nop().then_inc(pool_waited, 1)
                pool.tensor_scalar(ln1[:, 0, :], ln1[:, 3, :], EPS, 1.0, ALU.add, ALU.mult).then_inc(ln1_step, 1)
                pool.wait_ge(ln1_step, s + 5)
                pool.tensor_tensor(ln1[:, 2, :], ln1[:, 0, :], mhalf[:, 0:TT], ALU.pow).then_inc(ln1_step, 1)

            def coefficients1_third(mean, s):
                pool.wait_ge(ln1_step, s + 6)
                pool.tensor_tensor(ln1[:, 4, :], ln1[:, 1, :], ln1[:, 2, :], ALU.mult).then_inc(ln1_step, 1)
                pool.wait_ge(ln1_step, s + 7)
                pool.tensor_tensor(ln1[:, 3, :], mean, ln1[:, 4, :], ALU.mult).then_inc(ln1_step, 1)
                pool.wait_ge(ln1_step, s + 8)
                pool.nop().then_inc(pool_waited, 1)
                pool.tensor_scalar(ln1[:, 5, :], ln1[:, 3, :], -1.0, 0.0, ALU.mult, ALU.add).then_inc(ln1_step, 1)
                pool.wait_ge(ln1_step, s + 9)

            def normalise(tt):
                pool.nop().then_inc(pool_waited, 1)
                pool.tensor_scalar(xn[:, tt, :], xn[:, tt, :], ln1[:, 4, tt:tt + 1], ln1[:, 5, tt:tt + 1],
                                   ALU.mult, ALU.add).then_inc(norm1, 1)

            def residual(t, half, tt):
                pool.wait_ge(dv_free, t.pv + TT * half + tt + 1)
                part = x1[:, tt, D // 2 * half:D // 2 * (half + 1)]
                pool.tensor_tensor(part, part, y_half[tt], ALU.add).then_inc(x1_sum if half else x1_half, 1)

            def coefficients2(t, half):
                a, b = 2 * half, 2 * half + 2
                s = LN2_STEPS * t.k + 4 * half
                pool.wait_ge(st2_done, 2 * t.k + half + 1)
                pool.nop().then_inc(pool_waited, 1)
                pool.tensor_scalar(ln2[:, 0, a:b], mv2[:, a:b, 1], EPS, 1.0, ALU.add, ALU.mult).then_inc(ln2_step, 1)
                pool.wait_ge(ln2_step, s + 1)
                pool.tensor_tensor(ln2[:, 1, a:b], ln2[:, 0, a:b], mhalf[:, a:b], ALU.pow).then_inc(ln2_step, 1)
                if half == 0:
                    pool.wait_ge(ln2_step, s + 2)
                    pool.tensor_tensor(ln2[:, 2, a:b], mv2[:, a:b, 0], ln2[:, 1, a:b], ALU.mult).then_inc(ln2_step, 1)
                    pool.wait_ge(ln2_step, s + 3)
                    pool.nop().then_inc(pool_waited, 1)
                    pool.tensor_scalar(ln2[:, 3, a:b], ln2[:, 2, a:b], -1.0, 0.0, ALU.mult,
                                       ALU.add).then_inc(ln2_step, 1)

            pool.memset(mhalf[:], -0.5)
            pool.memset(ident[:], 0.0).then_inc(const_step, 1)
            pool.wait_ge(const_step, 1)
            pool.affine_select(out=ident[:], in_=ident[:], compare_op=ALU.not_equal, fill=1.0, base=0,
                               pattern=[[-1, P]], channel_multiplier=1).then_inc(consts, 1)
            pool.memset(kbd[:].bitcast(F32), 0.0).then_inc(cleared, 1)
            pool.wait_ge(cleared, 1)
            pool.memset(ks[3 * HD:KS].bitcast(F32), 1.0).then_inc(cleared, 1)
            pool.wait_ge(ctx_stats, 2)
            pool.tensor_scalar(ln2[0:N, 0, 0:B], mv2[0:N, 0:B, 1], EPS, 1.0, ALU.add, ALU.mult).then_inc(ctx_coef, 1)
            pool.wait_ge(ctx_coef, 1)
            pool.tensor_tensor(ln2[0:N, 1, 0:B], ln2[0:N, 0, 0:B], mhalf[0:N, 0:B], ALU.pow).then_inc(ctx_coef, 1)
            pool.wait_ge(st1_done, 1)
            coefficients1(0)
            for tt in range(TT // 2):
                normalise(tt)
            pool.wait_ge(cleared, 2)
            pool.memset(vs[:, :, 0, HD:VW], 1.0)
            pool.memset(vs[:, :, 1:3, HD:VW], 0.0)
            pool.wait_ge(wq_lo, 1)
            pool.wait_ge(setup_pe, LC + 1)
            pool.memset(v_other[:, :, 0, HD:VW], 1.0)
            pool.memset(v_other[:, :, 1:3, HD:VW], 0.0).then_inc(cleared, 1)
            for n, (w, w_raw) in enumerate(((u1, u1_raw), (v2, v2_raw), (u2, u2_raw), (v1, v1_raw))):
                if n == 2:
                    pool.wait_ge(st1_done, 2)
                    coefficients1(1)
                    for tt in range(TT // 2):
                        normalise(tt)
                pool.wait_ge(w_hi, n + 1)
                pool.tensor_tensor(w[:, 1], w_raw, w[:, 0].bitcast(F32), ALU.subtract).then_inc(w_lo, 1)

            def body(t):
                k = t.k
                for h in range(0, HEADS, 2):
                    if h % 4:
                        pool.wait_ge(ph_done, PH * k + 3 * (h // 4) + h % 4)
                    else:
                        pool.wait_ge(sc_done, t.sb + h + 1)
                    hi, lo = (pw[0:N, i, TB * h:TB * (h + 1)] for i in range(2))
                    pool.tensor_tensor(lo, pt[:, h % 4, :], hi, ALU.subtract).then_inc(pl_even, 1)
                pool.wait_ge(x1_in, DMA * (k + 1))
                for tt in range(TT):
                    residual(t, 0, tt)
                for tt in range(TT - 1):
                    residual(t, 1, tt)
                coefficients2(t, 0)
                coefficients2(t, 1)
                for n in range(FC // 2):
                    f = 2 * n
                    pool.wait_ge(sc_done, t.v1 + f + 1)
                    pool.tensor_tensor(x1t[:, 1, f % 4, :], ql[:, f % 4, :], x1t[:, 0, f % 4, :].bitcast(F32),
                                       ALU.subtract).then_inc(h_even, 1)
                    if 3 <= n < 6 and t.has_x:
                        if n == 3:
                            pool.wait_ge(st1_done, k + 3)
                        coefficients1(k + 2, n - 3)
                    if n in (0, 1, 2, 5):
                        tt = min(n, TT - 1)
                        if n == 0:
                            pool.wait_ge(norm2_act, t.norm2)
                            pool.wait_ge(norm2_dve, t.norm2)
                            if t is first:
                                pool.wait_ge(row_in, DMA * 2)
                        pool.tensor_tensor(x1[:, tt, :], x1[:, tt, :], b2_all[:], ALU.add).then_inc(x1_b2, 1)

            run(pool, body)


_INS = ['x', 'ctx_768', 'L0_xattn_norm_g', 'L0_xattn_norm_b', 'L0_xattn_tnorm_g', 'L0_xattn_tnorm_b',
        'L0_xattn_Wq', 'L0_xattn_bq', 'L0_xattn_Wk', 'L0_xattn_bk', 'L0_xattn_Wv', 'L0_xattn_bv',
        'L0_ffn_U1', 'L0_ffn_V1', 'L0_ffn_b1', 'L0_ffn_U2', 'L0_ffn_V2', 'L0_ffn_b2']
_CHUNKED = {'L0_xattn_norm_g', 'L0_xattn_norm_b', 'L0_xattn_tnorm_g', 'L0_xattn_tnorm_b', 'L0_xattn_bq',
            'L0_xattn_bk', 'L0_ffn_b1'}


def kernel(**inputs):
    import numpy as _np
    import concourse.bacc as _bacc
    from concourse import mybir as _mybir
    from concourse.bass_utils import run_bass_kernel_spmd as _run

    nc = _bacc.Bacc("TRN2", target_bir_lowering=False, num_devices=1)
    arrays, args = {}, []
    for name in _INS:
        a = _np.asarray(inputs[name])
        if name in _CHUNKED:
            a = a.reshape(-1, 128).T
        a = _np.ascontiguousarray(a)
        arrays[f"in_{name}"] = a
        args.append(nc.dram_tensor(f"in_{name}", a.shape, _mybir.dt.from_np(a.dtype), kind="ExternalInput").ap())
    shape = _np.asarray(inputs['x']).shape
    args.append(nc.dram_tensor("out_0", shape, _mybir.dt.float32, kind="ExternalOutput").ap())
    xattn_ffn(nc, *args)
    r = _run(nc, [arrays], core_ids=[0])
    return r.results[0]["out_0"]
```
